# Optimizing a Trainium2 kernel written in Bass

```python
import numpy as np
import jax
import jax.numpy as jnp

def _softmax(x, axis=-1):
    return jax.nn.softmax(x, axis=axis)

def _gelu(x):
    return jax.nn.gelu(x, approximate=True)

def _silu(x):
    return jax.nn.silu(x)

def _sigmoid(x):
    return jax.nn.sigmoid(x)

def _layernorm(x, axis=-1, eps=1e-05):
    m = jnp.mean(x, axis=axis, keepdims=True)
    v = jnp.var(x, axis=axis, keepdims=True)
    return (x - m) / jnp.sqrt(v + eps)

def _scatter_add(tgt, idx, src, axis=0):
    return tgt.at[idx].add(src)

def _segment_sum(src, seg, n):
    return jax.ops.segment_sum(src, seg, n)
kernel_name = 'mk_adj_resnorm_d1_adj_r2_649efa'

def setup_inputs(seed: int=0):
    np.random.seed(seed)
    _w = jnp.asarray

    def _rec_inputs():
        import jax
        import jax.numpy as jnp
        _gk = jax.random.key(seed)
        x = -0.000929 + 1 * jax.random.normal(jax.random.fold_in(_gk, 1), (8192, 128), jnp.float32)
        _w = (1.0 + jnp.arange(8192, dtype=jnp.float32)) ** (-0.5)
        _w = _w / _w.mean()
        _pij = jnp.clip(0.00195312 * _w[:, None] * _w[None, :], 0.0, 1.0)
        _a = jax.random.uniform(jax.random.fold_in(_gk, 2), (8192, 8192)) < _pij
        _af = _a.astype(jnp.float32)
        adj = _af
        return (x, adj)
    x, adj = _rec_inputs()

    def _L0_gnn_setup():
        import jax, jax.numpy as jnp
        import numpy as np
        N, IN_DIM, OUT_DIM, HEADS = (2048, 128, 128, 4)
        D_K = OUT_DIM // HEADS
        NEG_SLOPE = 0.2
        key = jax.random.key(seed)
        k1, k2, k3, k4, k5 = jax.random.split(key, 5)
        H = jax.random.normal(k1, (N, IN_DIM), dtype=jnp.float32)
        A = jax.random.randint(k2, (N, N), 0, 2).astype(jnp.float32)
        W = jax.random.normal(k3, (OUT_DIM, IN_DIM), dtype=jnp.float32) * (1.0 / np.sqrt(IN_DIM))
        a_l = jax.random.normal(k4, (HEADS, D_K), dtype=jnp.float32) * 0.1
        a_r = jax.random.normal(k5, (HEADS, D_K), dtype=jnp.float32) * 0.1
        return {'H': H, 'A': A, 'W': W, 'a_l': a_l, 'a_r': a_r}
    _L0_gnn_all = _L0_gnn_setup()
    _L0_gnn_in = {k: v for k, v in _L0_gnn_all.items() if k in ('W', 'a_l', 'a_r')}
    del _L0_gnn_all
    return {'x': x, 'adj': adj, 'L0_gnn_W': _L0_gnn_in['W'], 'L0_gnn_a_l': _L0_gnn_in['a_l'], 'L0_gnn_a_r': _L0_gnn_in['a_r']}

def reference(x, adj, L0_gnn_W, L0_gnn_a_l, L0_gnn_a_r):
    import jax
    import jax.numpy as jnp

    def _L0_gnn_ref(H, A, W, a_l, a_r):
        import jax, jax.numpy as jnp
        import numpy as np
        N, IN_DIM, OUT_DIM, HEADS = (2048, 128, 128, 4)
        D_K = OUT_DIM // HEADS
        NEG_SLOPE = 0.2
        n = H.shape[0]
        A_tilde = A + jnp.eye(n, dtype=A.dtype)
        mask = A_tilde > 0
        Wh = (H @ W.T).reshape(n, HEADS, D_K)
        score_l = jnp.einsum('nhd,hd->nh', Wh, a_l)
        score_r = jnp.einsum('nhd,hd->nh', Wh, a_r)
        e = score_l[:, :, None] + score_r.T[None, :, :]
        e = jnp.where(e >= 0, e, NEG_SLOPE * e)
        e = jnp.where(mask[:, None, :], e, -jnp.inf)
        alpha = jax.nn.softmax(e, axis=2)
        out = jnp.einsum('nhm,mhd->nhd', alpha, Wh).reshape(n, OUT_DIM)
        return jax.nn.elu(out)
    x = _layernorm(x + _L0_gnn_ref(x, adj, L0_gnn_W, L0_gnn_a_l, L0_gnn_a_r), axis=-1)
    return x

_drawn_inputs = setup_inputs


def setup_inputs(seed=0):
    import zlib

    import numpy as np

    out = dict(_drawn_inputs(seed))
    spreads = {}
    factors = {}
    for name, (base, spread) in spreads.items():
        noise = np.random.default_rng([zlib.crc32(name.encode()), seed]).standard_normal(out[name].shape)
        drawn = base * np.exp(spread * noise) if base else spread * noise
        out[name] = jnp.asarray(drawn.astype(out[name].dtype))
    for name, factor in factors.items():
        out[name] = (out[name] * factor).astype(out[name].dtype)
    return out
```

```python
import numpy as np
import concourse.bass as bass
from concourse import mybir
from contextlib import ExitStack


def gat_kernel(nc, x, adj, W, a_l, a_r, out):
    fp32, bf16, fp8, i32 = mybir.dt.float32, mybir.dt.bfloat16, mybir.dt.float8e4, mybir.dt.int32
    ALU, ACT, AX = mybir.AluOpType, mybir.ActivationFunctionType, mybir.AxisListType
    P = 128
    N, D = x.shape
    H, DK = a_l.shape
    SLOPE, EPS = 0.2, 1e-5
    NT = N // P
    J = 4
    CN = J * P
    NCH = N // CN
    PAIRS = 4
    TURNS = NCH // 2
    CP = PAIRS * TURNS
    E = DK + 1
    S3 = 3 * E
    ITEMS = H * J * 2
    PB = 512 // S3
    BANKS = -(-ITEMS // PB)
    DW = D + 2 * H
    BIG = 2.0 ** 100
    ONE8 = 0x38383838
    SHARED = 5152
    HALF = H // 2

    ctx = ExitStack()
    with ctx:
        def sb(name, shape, dt):
            return ctx.enter_context(nc.sbuf_tensor(name, shape, dt))

        def sem(name):
            return ctx.enter_context(nc.semaphore(name))

        l_dram = nc.dram_tensor("l_scratch", [NCH, H * J, P], fp32, kind="Internal").ap()

        vtab = sb("vtab", [P, NT, 2 * H * S3], bf16)
        abuf = sb("abuf", [P, 2, J, CN], fp32)
        lnext = sb("lnext", [P, H, CN], fp32)
        lrow = sb("lrow", [P, H, CN], fp32)
        MB = H * 2 * CN // 4
        VB = 2 * 2 * H * S3 // 2
        work = sb("work", [P, max(NT * DW, 6 * MB + 4 * VB)], fp32)
        wh = work[:, 0:NT * DW].rearrange("p (t w) -> p t w", w=DW)
        bmask = work[:, 0:4 * MB].bitcast(fp8).rearrange("p (s h n) -> p s h n", s=4, h=H)
        cmask = work[:, 4 * MB:6 * MB].bitcast(fp8).rearrange("p (s h n) -> p s h n", s=2, h=H)
        vring = work[:, 6 * MB:6 * MB + 4 * VB].bitcast(bf16).rearrange("p (s i e) -> p s i e", s=4, i=2)
        amask = sb("amask", [P, 4, 2 * CN], fp8)
        identf = sb("identf", [P, P], fp32)
        identb = sb("identb", [P, P], bf16)
        w_nat = sb("w_nat", [P, P], fp32)
        w_t = sb("w_t", [P, DW], fp32)
        acol = sb("acol", [P, 2], fp32)
        ablk = sb("ablk", [P, 2 * H], fp32)
        shared = sb("shared", [P, SHARED], fp32)
        used = {"early": 0, "late": 0}

        def carve(when, shape):
            size = int(np.prod(shape))
            at = used[when]
            used[when] += size
            assert used[when] <= SHARED
            names = [f"d{i}" for i in range(len(shape))]
            return shared[:, at:at + size].rearrange(f"p ({' '.join(names)}) -> p {' '.join(names)}",
                                                     **dict(zip(names, shape)))

        def early(*shape):
            return carve("early", shape)

        def late(*shape):
            return carve("late", shape)

        xs = early(2, J, P)
        x_t = early(2, CN)
        used["early"] = 2 * 2 * 2 * H * 2 * E
        rmax1 = sb("rmax1", [P, H], fp32)
        rmax = sb("rmax", [P, H], fp32)
        rtab = sb("rtab", [P, NT, 2 * H], fp32)
        rring = sb("rring", [P, PAIRS, 2, 2 * H], fp32)
        dr = early(NT, H)
        tl = early(NT, H)
        um = early(2, NT, H)
        lcols = early(NT * H)
        l_t = early(2, P)
        vv = early(NT, H, 2)
        uu = sb("uu", [P, NCH, ITEMS], fp32)
        used["early"] = 0
        vf = early(2, 2 * H * 2, E)
        vr = early(2, 2 * H * 2, E)
        acc = late(ITEMS, E)
        dn = sb("dn", [P, ITEMS], fp32)
        den = sb("den", [P, ITEMS // 2], fp32)
        rden = sb("rden", [P, ITEMS // 2], fp32)
        wgt = sb("wgt", [P, ITEMS], fp32)
        pm = late(ITEMS, DK)
        ov = late(J, P)
        mn = late(J, P)
        em = late(J, P)
        zz = late(J, P)
        xr = late(J, P)
        st = sb("st", [P, J, 6], fp32)
        mv = sb("mv", [P, J, 2], fp32)
        epsc = sb("epsc", [P, 2 * J], fp32)
        vrs = sb("vrs", [P, J], fp32)
        yout = late(J, P)

        psum = ctx.enter_context(nc.psum_tensor("psum", [P, BANKS, 512], fp32))
        trp = ctx.enter_context(nc.psum_tensor("trp", [P, 2, CN], bf16))

        consts_zero, consts, w_in, a_in = sem("consts_zero"), sem("consts"), sem("w_in"), sem("a_in")
        w_tr, w_copied, ablk_done, wa_done, wt_done = (sem(s) for s in ("w_tr", "w_copied", "ablk_done", "wa_done", "wt_done"))
        x_in = [sem("x_in0"), sem("x_in1")]
        x_tr, x_copied, wh_done, wh_copied = sem("x_tr"), sem("x_copied"), sem("wh_done"), sem("wh_copied")
        rmax1_done, rmax_done, tab_step, tab_done = sem("rmax1_done"), sem("rmax_done"), sem("tab_step"), sem("tab_done")
        exp_done, l_tr, l_copied, l_stored = sem("exp_done"), sem("l_tr"), sem("l_copied"), sem("l_stored")
        v_prod, v_hi, v_rest, v_mid, v_lo = (sem(s) for s in ("v_prod", "v_hi", "v_rest", "v_mid", "v_lo"))
        a_loaded = [sem("a_loaded0"), sem("a_loaded1")]
        diag_done, tr_done, evac_done = sem("diag_done"), sem("tr_done"), sem("evac_done")
        v_in = [sem(f"v_in{k}") for k in range(PAIRS)]
        r_ready, lrow_act, lrow_dve = sem("r_ready"), sem("lrow_act"), sem("lrow_dve")
        lrow_in, cmp_act, cmp_dve = sem("lrow_in"), sem("cmp_act"), sem("cmp_dve")
        b_ready, c_ready, mm_done, bank_free = sem("b_ready"), sem("c_ready"), sem("mm_done"), sem("bank_free")
        acc_read, dn_step, w_ready = bank_free, sem("dn_step"), sem("w_ready")
        pool_step, mn_ready, em_ready, zz_ready, z_step = (sem(s) for s in ("pool_step", "mn_ready", "em_ready", "zz_ready", "z_step"))
        mv_ready, y_ready, y_stored, xr_in = sem("mv_ready"), sem("y_ready"), sem("y_stored"), sem("xr_in")

        passed = {str(e): sem(f"passed{i}") for i, e in enumerate(
            (nc.sync.engine, nc.tensor.engine, nc.scalar.engine, nc.vector.engine, nc.gpsimd.engine))}
        POOL_STEPS = 5

        block = ctx.enter_context(nc.Block())

        def wait(eng, s, value):
            if not (isinstance(value, int) and value <= 0):
                eng.wait_ge(s, value)

        def repeat(eng, count, body):
            body(0)
            with eng.Fori(1, count) as i:
                body(i)

        def settle(eng):
            eng.sem_inc(passed[str(eng.engine)], 1)

        def group_of(c, t, s):
            return (c + 2 * t + s) & (NCH - 1)

        @block.sync
        def _(sp):
            sp.dma_start(w_nat[:, :], W[:, :]).then_inc(w_in, 16)
            sp.dma_start(acol[:, 0:1], a_l.rearrange("h (k o) -> (h k) o", o=1)).then_inc(a_in, 16)
            sp.dma_start(acol[:, 1:2], a_r.rearrange("h (k o) -> (h k) o", o=1)).then_inc(a_in, 16)

            def x_group(i):
                for s in range(2):
                    g = 2 * i + s
                    wait(sp, x_tr, g - 1)
                    settle(sp)
                    src = x[bass.ds(g * CN, CN), :].rearrange("(j p) d -> p j d", p=P)
                    sp.dma_start(xs[:, s], src).then_inc(x_in[s], 16)

            def a_group(c, t, s):
                q = NCH * c + 2 * t + s
                wait(sp, tr_done, 2 * (q - 1))
                settle(sp)
                col = group_of(c, t, s) * CN
                src = adj[bass.ds(c * CN, CN), bass.ds(col, CN)].rearrange("(j p) m -> p j m", p=P)
                sp.dma_start(abuf[:, s], src).then_inc(a_loaded[s], 16)

            def load_lrow(c):
                src = l_dram[bass.ds(c, 1)].rearrange("o i p -> o (i p)").to_broadcast([P, H * CN])
                sp.dma_start(lnext.rearrange("p h n -> p (h n)"), src).then_inc(lrow_in, 16)

            def loads(c, t):
                for s in range(2):
                    a_group(c, t, s)

            def rest_of_chunk(c, first):
                with sp.Fori(1, 3) as t:
                    loads(c, t)
                sp.wait_ge(lrow_act, c + 1)
                sp.wait_ge(lrow_dve, c + 1)
                settle(sp)
                load_lrow((c + 1) & (NCH - 1))
                wait(sp, zz_ready, c)
                if first:
                    sp.wait_ge(v_lo, NT // 2)
                settle(sp)
                sp.dma_start(xr[:, :], x[bass.ds(c * CN, CN), :].rearrange("(j p) d -> p j d", p=P)).then_inc(xr_in, 16)
                if not first:
                    sp.wait_ge(y_ready, c)
                    settle(sp)
                    store_y(c - 1)
                with sp.Fori(3, TURNS) as t:
                    loads(c, t)

            def store_y(c):
                sp.dma_start(out[bass.ds(c * CN, CN), :].rearrange("(j p) d -> p j d", p=P), yout[:, :]).then_inc(y_stored, 16)

            repeat(sp, NCH // 2, x_group)
            a_group(0, 0, 0)
            a_group(0, 0, 1)
            sp.wait_ge(l_copied, 1)
            sp.dma_start(l_dram.rearrange("(a c) i p -> (c i) a p", a=2), l_t[:, :]).then_inc(l_stored, 16)
            sp.wait_ge(l_stored, 16)
            load_lrow(0)
            rest_of_chunk(0, True)
            with sp.Fori(1, NCH) as c:
                loads(c, 0)
                rest_of_chunk(c, False)
            for s in range(2):
                sp.wait_ge(tr_done, 2 * (NCH * NCH - 1 + s))
                sp.dma_start(abuf[:, s], adj[0:CN, 0:CN].rearrange("(j p) m -> p j m", p=P)).then_inc(a_loaded[s], 16)
            sp.wait_ge(y_ready, NCH)
            store_y(NCH - 1)
            sp.wait_ge(y_stored, 16 * NCH)

        @block.tensor
        def _(pe):
            pe.wait_ge(consts, 2)
            pe.wait_ge(w_in, 16)
            nc.tensor.transpose(psum[:, BANKS - 1, 0:P], w_nat[:, :], identf[:, :]).then_inc(w_tr, 1)
            pe.wait_ge(ablk_done, 1)
            nc.tensor.matmul(psum[:, BANKS - 2, 0:2 * H], w_nat[:, :], ablk[:, :], start=True, stop=True).then_inc(wa_done, 1)
            pe.wait_ge(wt_done, 2)

            def project(i):
                for s in range(2):
                    g = 2 * i + s
                    pe.wait_ge(x_in[s], 16 * (i + 1))
                    wait(pe, x_copied, g - 1)
                    for j in range(J):
                        last = nc.tensor.transpose(psum[:, s, j * P:(j + 1) * P], xs[:, s, j], identf[:, :])
                    last.then_inc(x_tr, 1)
                for s in range(2):
                    g = 2 * i + s
                    pe.wait_ge(x_copied, g + 1)
                    wait(pe, wh_copied, 2 * (g - 1))
                    for j in range(J):
                        last = nc.tensor.matmul(psum[:, 2 + 2 * s + j // 2, (j % 2) * DW:(j % 2 + 1) * DW],
                                                x_t[:, s, j * P:(j + 1) * P], w_t[:, :], start=(j % 2 == 0), stop=True,
                                                skip_group_check=True)
                    last.then_inc(wh_done, 1)

            repeat(pe, NCH // 2, project)
            pe.wait_ge(tab_step, 1)
            for a in range(2):
                last = nc.tensor.transpose(psum[:, BANKS - 1, a * P:(a + 1) * P], lcols[:, a * P:(a + 1) * P], identf[:, :])
            last.then_inc(l_tr, 1)

            def transposes(c, t, k):
                q = 4 * (TURNS * c + t) + k
                kk, tt = k % 4, t + k // 4
                s = kk // 2
                if kk % 2 == 0:
                    pe.wait_ge(a_loaded[s], 16 * (TURNS * c + tt + 1))
                if kk == 0:
                    pe.wait_ge(diag_done, ((TURNS * c + tt) >> 3) + 1)
                wait(pe, evac_done, q)
                for i in range(2):
                    m = (2 * (kk % 2) + i) * P
                    for j in range(J):
                        block_hi = abuf[:, s, j, m:m + P].bitcast(bf16)[:, 1::2]
                        last = nc.tensor.transpose(trp[:, i, j * P:(j + 1) * P], block_hi, identb[:, :])
                last.then_inc(tr_done, 1)

            def products(c, t, k, first_turn):
                q = 4 * (TURNS * c + t) + k
                pe.wait_ge(v_in[k], 16 * (TURNS * c + t + 1))
                for half in range(2):
                    pe.wait_ge(b_ready, 2 * q + half + 1)
                    pe.wait_ge(c_ready, 2 * q + half + 1)
                    settle(pe)
                    for i in range(2):
                        for h in range(half * HALF, (half + 1) * HALF):
                            for j in range(J):
                                for b, (mask, slots) in enumerate(((bmask, 4), (cmask, 2))):
                                    item = (h * J + j) * 2 + b
                                    bank, at = item // PB, item % PB
                                    opens = first_turn and k == 0 and i == 0 and at == 0
                                    if opens and not isinstance(c, int):
                                        pe.wait_ge(bank_free, BANKS * (c - 1) + bank + 1)
                                        settle(pe)
                                    col = (h * 2 + b) * S3
                                    last = nc.tensor.matmul(
                                        psum[:, bank, at * S3:(at + 1) * S3],
                                        mask[:, k % slots, h, i * CN + j * P:i * CN + (j + 1) * P],
                                        vring[:, k, i, col:col + S3],
                                        start=opens, stop=True, skip_group_check=True)
                last.then_inc(mm_done, 1)

            def turn(c, t, first_turn):
                for k in range(PAIRS):
                    transposes(c, t, k + 3)
                    products(c, t, k, first_turn)

            def chunk(c):
                turn(c, 0, True)
                with pe.Fori(1, TURNS) as t:
                    turn(c, t, False)

            transposes(0, 0, 0)
            transposes(0, 0, 1)
            transposes(0, 0, 2)
            pe.wait_ge(v_lo, NT // 2)
            pe.wait_ge(wh_copied, 2 * NCH)
            chunk(0)
            with pe.Fori(1, NCH) as c:
                chunk(c)

        @block.scalar
        def _(act):
            def copy_wh(i):
                for s in range(2):
                    g = 2 * i + s
                    act.wait_ge(wh_done, g + 1)
                    for b in range(2):
                        nc.scalar.copy(wh[:, bass.ds(g * J + 2 * b, 2), :].rearrange("p t w -> p (t w)"),
                                       psum[:, 2 + 2 * s + b, 0:2 * DW]).then_inc(wh_copied, 1)

            repeat(act, NCH // 2, copy_wh)
            act.wait_ge(tab_step, 3)
            for b, scale in enumerate((1.0, SLOPE)):
                nc.scalar.activation(vv[:, :, :, b], dr[:, :, :], ACT.Exp, scale=scale).then_inc(exp_done, 1)
            act.wait_ge(tab_done, 1)
            for b in range(2):
                nc.scalar.activation(uu.rearrange("p c (h j b) -> p c j h b", h=H, b=2)[:, :, :, :, b].rearrange("p c j h -> p c j h"),
                                     um[:, b].rearrange("p (c j) h -> p c j h", j=J), ACT.Exp).then_inc(exp_done, 1)

            def split(i):
                for s in range(2):
                    g = 2 * i + s
                    dst = vtab[:, bass.ds(2 * g, 2), :].rearrange("p t (i e) -> p (t i) e", e=S3)
                    act.wait_ge(v_prod, g + 1)
                    nc.scalar.copy(dst[:, :, 0:E], vf[:, s]).then_inc(v_hi, 1)
                    act.wait_ge(v_rest, g + 1)
                    nc.scalar.copy(dst[:, :, E:2 * E], vr[:, s]).then_inc(v_mid, 1)

            repeat(act, NT // 4, split)

            def evacuate(c, t, k):
                q = 4 * (TURNS * c + t) + k
                act.wait_ge(tr_done, q + 1)
                wait(act, c_ready, 2 * (q - 3))
                settle(act)
                nc.scalar.activation(amask[:, k % 4], trp.rearrange("p i n -> p (i n)"), ACT.Relu,
                                     scale=BIG, saturate=False).then_inc(evac_done, 1)

            def compare(c, t, k):
                q = 4 * (TURNS * c + t) + k
                t, k = t + k // PAIRS, k % PAIRS
                wait(act, mm_done, q - 3)
                act.wait_ge(r_ready, 2 * (TURNS * c + t) + k // 2 + 1)
                settle(act)
                tile = group_of(c, t, k // 2) * J + 2 * (k % 2)
                act.dma_start(vring[:, k].rearrange("p i e -> p (i e)"),
                              vtab[:, bass.ds(tile, 2)].rearrange("p i e -> p (i e)")).then_inc(v_in[k], 16)
                for i in range(2):
                    for h in range(HALF):
                        last = nc.scalar.activation(bmask[:, k, h, i * CN:(i + 1) * CN], lrow[:, h], ACT.Relu,
                                                    bias=rring[:, k, i, H + h:H + h + 1], scale=BIG, saturate=False)
                last.then_inc(cmp_act, 1)

            def turn(c, t, first=False, last=False):
                for k in range(PAIRS):
                    evacuate(c, t, k + 2)
                    if not (last and k == PAIRS - 1):
                        compare(c, t, k + 1)
                    if first and k == 2 and not isinstance(c, int):
                        elu_exp(c)

            def elu_exp(c):
                act.wait_ge(mn_ready, c)
                nc.scalar.activation(em[:, :], mn[:, :], ACT.Exp).then_inc(em_ready, 1)

            def chunk(c):
                act.wait_ge(lrow_in, 16 * (c + 1))
                wait(act, cmp_act, CP * c)
                nc.scalar.copy(lrow[:, 0:HALF], lnext[:, 0:HALF]).then_inc(lrow_act, 1)
                act.wait_ge(lrow_act, c + 1)
                compare(c, 0, 0)
                turn(c, 0, first=True)
                with act.Fori(1, TURNS - 1) as t:
                    turn(c, t)
                turn(c, TURNS - 1, last=True)

            act.wait_ge(tab_done, 2)
            act.wait_ge(v_lo, NT // 2)
            evacuate(0, 0, 0)
            evacuate(0, 0, 1)
            chunk(0)
            with act.Fori(1, NCH) as c:
                chunk(c)
            elu_exp(NCH)

        @block.vector
        def _(dve):
            dve.wait_ge(consts_zero, 1)
            dve.wait_ge(a_in, 32)
            for h in range(H):
                last = nc.vector.tensor_copy(ablk[h * DK:(h + 1) * DK, h:h + H + 1:H], acol[h * DK:(h + 1) * DK, :])
            last.then_inc(ablk_done, 1)
            dve.wait_ge(w_tr, 1)
            nc.vector.tensor_copy(w_t[:, 0:P], psum[:, BANKS - 1, 0:P]).then_inc(wt_done, 1)
            dve.wait_ge(wa_done, 1)
            nc.vector.tensor_copy(w_t[:, P:DW], psum[:, BANKS - 2, 0:2 * H]).then_inc(wt_done, 1)

            def copy_xt(i):
                for s in range(2):
                    g = 2 * i + s
                    dve.wait_ge(x_tr, g + 1)
                    wait(dve, wh_done, g - 1)
                    nc.vector.tensor_copy(x_t[:, s], psum[:, s, :]).then_inc(x_copied, 1)

            repeat(dve, NCH // 2, copy_xt)
            dve.wait_ge(wh_copied, 2 * NCH)
            l_all, r_all = wh[:, :, D:D + H], wh[:, :, D + H:DW]
            nc.vector.tensor_copy(lcols.rearrange("p (c h j) -> p c h j", h=H, j=J),
                                  l_all.rearrange("p (c j) h -> p c h j", j=J)).then_inc(tab_step, 1)
            nc.vector.tensor_reduce(rmax1[:, :], r_all.rearrange("p t h -> p h t"), AX.X, ALU.max).then_inc(rmax1_done, 1)
            nc.vector.tensor_scalar(rtab[:, :, 0:H], r_all, -1.0, None, ALU.mult).then_inc(tab_step, 1)
            nc.vector.tensor_scalar(rtab[:, :, H:2 * H], r_all, BIG, None, ALU.mult)
            dve.wait_ge(rmax_done, 1)
            r_top = rmax.rearrange("p (o h) -> p o h", o=1).to_broadcast([P, NT, H])
            nc.vector.tensor_tensor(dr[:, :, :], r_all, r_top, ALU.subtract).then_inc(tab_step, 1)
            nc.vector.tensor_tensor(tl[:, :, :], l_all, r_top, ALU.add).then_inc(tab_step, 1)
            dve.wait_ge(tab_step, 4)
            nc.vector.tensor_scalar(um[:, 0], tl[:, :, :], 1.0 - SLOPE, 0.0, ALU.mult, ALU.min)
            nc.vector.tensor_scalar(um[:, 1], tl[:, :, :], SLOPE - 1.0, 0.0, ALU.mult, ALU.min).then_inc(tab_done, 1)
            dve.wait_ge(l_tr, 1)
            nc.vector.tensor_copy(l_t.rearrange("p a n -> p (a n)"), psum[:, BANKS - 1, 0:2 * P]).then_inc(l_copied, 1)

            def split(i):
                for s in range(2):
                    g = 2 * i + s
                    dst = vtab[:, bass.ds(2 * g, 2), :].rearrange("p t (i e) -> p (t i) e", e=S3)
                    dve.wait_ge(v_hi, g + 1)
                    wait(dve, v_lo, g - 1)
                    nc.vector.tensor_tensor(vr[:, s], vf[:, s], dst[:, :, 0:E], ALU.subtract).then_inc(v_rest, 1)
                for s in range(2):
                    g = 2 * i + s
                    dst = vtab[:, bass.ds(2 * g, 2), :].rearrange("p t (i e) -> p (t i) e", e=S3)
                    dve.wait_ge(v_mid, g + 1)
                    nc.vector.tensor_tensor(dst[:, :, 2 * E:S3], vr[:, s], dst[:, :, E:2 * E], ALU.subtract).then_inc(v_lo, 1)

            repeat(dve, NT // 4, split)
            dve.wait_ge(v_lo, NT // 2)
            nc.vector.memset(epsc[:, 0:J], EPS)
            nc.vector.memset(epsc[:, J:2 * J], -0.5).then_inc(tab_done, 1)

            def words(ap):
                return ap.bitcast(i32)

            def masks(c, t, k):
                q = 4 * (TURNS * c + t) + k
                wait(dve, mm_done, q - 3)
                dve.wait_ge(r_ready, 2 * (TURNS * c + t) + k // 2 + 1)
                settle(dve)
                for i in range(2):
                    for h in range(HALF, H):
                        last = nc.vector.tensor_scalar(bmask[:, k, h, i * CN:(i + 1) * CN], lrow[:, h],
                                                       rring[:, k, i, h:h + 1], None, ALU.is_ge, saturate=False)
                last.then_inc(cmp_dve, 1)
                a_words = words(amask[:, k]).rearrange("p (o n) -> p o n", o=1).to_broadcast([P, HALF, 2 * CN // 4])
                dve.wait_ge(evac_done, q + 1)
                for half, done in enumerate((cmp_act, cmp_dve)):
                    dve.wait_ge(done, q + 1)
                    b_words = words(bmask[:, k, half * HALF:(half + 1) * HALF])
                    nc.vector.scalar_tensor_tensor(b_words, b_words, ONE8, a_words, ALU.bitwise_and,
                                                   ALU.bitwise_and).then_inc(b_ready, 1)
                wait(dve, mm_done, q - 1)
                for half in range(2):
                    dve.wait_ge(b_ready, 2 * q + half + 1)
                    nc.vector.scalar_tensor_tensor(words(cmask[:, k % 2, half * HALF:(half + 1) * HALF]), a_words, ONE8,
                                                   words(bmask[:, k, half * HALF:(half + 1) * HALF]),
                                                   ALU.bitwise_and, ALU.bitwise_xor).then_inc(c_ready, 1)

            def take_sums(c):
                dve.wait_ge(mm_done, CP * (c + 1))
                if not (isinstance(c, int) and c == 0):
                    dve.wait_ge(pool_step, POOL_STEPS * c)
                for b in range(BANKS):
                    n = min(PB, ITEMS - b * PB)
                    nc.vector.tensor_reduce(acc[:, b * PB:b * PB + n],
                                            psum[:, b, 0:n * S3].rearrange("p (i s e) -> p i e s", s=3, e=E),
                                            AX.X, ALU.add).then_inc(bank_free, 1)
                dve.wait_ge(bank_free, BANKS * (c + 1))
                u_c = uu[:, c] if isinstance(c, int) else uu[:, bass.ds(c, 1)].rearrange("p o i -> p (o i)")
                nc.vector.tensor_tensor(dn[:, :], acc[:, :, DK], u_c, ALU.mult).then_inc(dn_step, 1)
                dve.wait_ge(dn_step, 3 * c + 1)
                nc.vector.tensor_reduce(den[:, :], dn.rearrange("p (i b) -> p i b", b=2), AX.X, ALU.add).then_inc(dn_step, 1)
                dve.wait_ge(dn_step, 3 * c + 2)
                nc.vector.reciprocal(rden[:, :], den[:, :]).then_inc(dn_step, 1)
                dve.wait_ge(dn_step, 3 * c + 3)
                nc.vector.tensor_tensor(wgt.rearrange("p (i b) -> p i b", b=2), u_c.rearrange("p (i b) -> p i b", b=2),
                                        rden.rearrange("p (i o) -> p i o", o=1).to_broadcast([P, ITEMS // 2, 2]),
                                        ALU.mult).then_inc(w_ready, 1)

            def statistics(c):
                dve.wait_ge(em_ready, c + 1)
                dve.wait_ge(zz_ready, c + 1)
                nc.vector.scalar_tensor_tensor(ov[:, :], em[:, :], -1.0, zz[:, :], ALU.add, ALU.add).then_inc(z_step, 1)
                dve.wait_ge(z_step, 2 * c + 1)
                for j in range(J):
                    last = nc.vector.bn_stats(st[:, j], ov[:, j])
                last.then_inc(z_step, 1)
                dve.wait_ge(z_step, 2 * c + 2)
                settle(dve)
                for j in range(J):
                    last = nc.vector.bn_aggr(mv[:, j], st[:, j])
                last.then_inc(mv_ready, 1)

            def turn(c, t, first_turn):
                if first_turn:
                    dve.wait_ge(lrow_in, 16 * (c + 1))
                    wait(dve, cmp_dve, CP * c)
                    nc.vector.tensor_copy(lrow[:, HALF:H], lnext[:, HALF:H]).then_inc(lrow_dve, 1)
                    dve.wait_ge(lrow_dve, c + 1)
                for k in range(PAIRS):
                    masks(c, t, k)
                    if first_turn and not isinstance(c, int):
                        if k == 0:
                            take_sums(c - 1)
                        if k == 3:
                            statistics(c - 1)

            def chunk(c):
                turn(c, 0, True)
                with dve.Fori(1, TURNS) as t:
                    turn(c, t, False)

            chunk(0)
            with dve.Fori(1, NCH) as c:
                chunk(c)
            take_sums(NCH - 1)
            statistics(NCH - 1)

        @block.gpsimd
        def _(pool):
            nc.gpsimd.memset(ablk[:, :], 0.0).then_inc(consts_zero, 1)
            nc.gpsimd.memset(identf[:, :], 0.0).then_inc(consts_zero, 1)
            pool.wait_ge(consts_zero, 2)
            nc.gpsimd.affine_select(out=identf[:, :], in_=identf[:, :], compare_op=ALU.not_equal, fill=1.0, base=0,
                                    pattern=[[-1, P]], channel_multiplier=1).then_inc(consts, 1)
            pool.wait_ge(consts, 1)
            nc.gpsimd.tensor_copy(identb[:, :], identf[:, :]).then_inc(consts, 1)
            pool.wait_ge(rmax1_done, 1)
            nc.gpsimd.partition_all_reduce(rmax[:, :], rmax1[:, :], P, bass.bass_isa.ReduceOp.max).then_inc(rmax_done, 1)

            def product(i):
                for s in range(2):
                    g = 2 * i + s
                    wait(pool, v_rest, g - 1)
                    v4 = vf[:, s].rearrange("p (t h b) e -> p t h b e", t=2, b=2)
                    w3 = wh[:, bass.ds(2 * g, 2), 0:D].rearrange("p t (h d) -> p t h d", h=H)
                    for b in range(2):
                        vb = vv[:, bass.ds(2 * g, 2), :, b]
                        nc.gpsimd.tensor_tensor(v4[:, :, :, b, 0:DK], w3, vb.rearrange("p t (h o) -> p t h o", o=1).to_broadcast([P, 2, H, DK]),
                                                ALU.mult)
                    nc.gpsimd.tensor_copy(vf[:, s, :, DK], vv[:, bass.ds(2 * g, 2)].rearrange("p t h b -> p (t h b)")).then_inc(v_prod, 1)

            pool.wait_ge(exp_done, 2)
            repeat(pool, NT // 4, product)

            def add_diagonal(c):
                pool.wait_ge(a_loaded[0], 16 * (TURNS * c + 1))
                row = abuf[:, 0].rearrange("p j n -> p (j n)")
                diag = bass.AP(row.tensor, row.offset, [row.ap[0], [CN + P, J], [1, P]])
                nc.gpsimd.tensor_tensor(diag, diag, identf.rearrange("p (o n) -> p o n", o=1).to_broadcast([P, J, P]),
                                        ALU.add).then_inc(diag_done, 1)

            def scores_of(c, t):
                for s in range(2):
                    free = 4 * (TURNS * c + t) + 2 * s - 2
                    wait(pool, cmp_act, free)
                    wait(pool, cmp_dve, free)
                    settle(pool)
                    nc.gpsimd.tensor_copy(rring[:, 2 * s:2 * s + 2].rearrange("p k i w -> p (k i w)"),
                                          rtab[:, bass.ds(group_of(c, t, s) * J, J)].rearrange("p i w -> p (i w)")).then_inc(r_ready, 1)

            def weigh_sums(c):
                base = POOL_STEPS * c
                pool.wait_ge(w_ready, c + 1)
                nc.gpsimd.tensor_tensor(pm[:, :], acc[:, :, 0:DK],
                                        wgt.rearrange("p (i o) -> p i o", o=1).to_broadcast([P, ITEMS, DK]),
                                        ALU.mult).then_inc(pool_step, 1)
                pool.wait_ge(pool_step, base + 1)
                p2 = pm.rearrange("p (h j b) d -> p h j b d", h=H, b=2)
                nc.gpsimd.tensor_tensor(ov.rearrange("p j (h d) -> p h j d", h=H), p2[:, :, :, 0], p2[:, :, :, 1],
                                        ALU.add).then_inc(pool_step, 1)
                pool.wait_ge(pool_step, base + 2)
                settle(pool)
                nc.gpsimd.tensor_scalar(mn[:, :], ov[:, :], 0.0, None, ALU.min).then_inc(mn_ready, 1)
                pool.wait_ge(mn_ready, c + 1)
                nc.gpsimd.tensor_tensor(zz[:, :], ov[:, :], mn[:, :], ALU.subtract).then_inc(pool_step, 1)
                pool.wait_ge(pool_step, base + 3)
                pool.wait_ge(xr_in, 16 * (c + 1))
                nc.gpsimd.tensor_tensor(zz[:, :], zz[:, :], xr[:, :], ALU.add).then_inc(zz_ready, 1)

            def normalise(c):
                base = POOL_STEPS * c
                pool.wait_ge(mv_ready, c + 1)
                nc.gpsimd.tensor_tensor(vrs[:, :], mv[:, :, 1], epsc[:, 0:J], ALU.add).then_inc(pool_step, 1)
                pool.wait_ge(pool_step, base + 4)
                nc.gpsimd.tensor_tensor(vrs[:, :], vrs[:, :], epsc[:, J:2 * J], ALU.pow)
                nc.gpsimd.tensor_tensor(pm[:, 0:J * P // DK].rearrange("p (j g) d -> p j (g d)", j=J), ov[:, :],
                                        mv[:, :, 0:1].to_broadcast([P, J, P]), ALU.subtract).then_inc(pool_step, 1)
                pool.wait_ge(pool_step, base + 5)
                if not (isinstance(c, int) and c == 0):
                    pool.wait_ge(y_stored, 16 * c)
                nc.gpsimd.tensor_tensor(yout[:, :], pm[:, 0:J * P // DK].rearrange("p (j g) d -> p j (g d)", j=J),
                                        vrs.rearrange("p (j o) -> p j o", o=1).to_broadcast([P, J, P]),
                                        ALU.mult).then_inc(y_ready, 1)

            pool.wait_ge(tab_done, 1)
            scores_of(0, 0)
            add_diagonal(0)
            with pool.Fori(1, TURNS) as t:
                scores_of(0, t)
            add_diagonal(1)
            with pool.Fori(1, NCH) as c:
                scores_of(c, 0)
                weigh_sums(c - 1)
                scores_of(c, 1)
                normalise(c - 1)
                with pool.Fori(2, TURNS) as t:
                    scores_of(c, t)
                add_diagonal(c + 1)
            weigh_sums(NCH - 1)
            normalise(NCH - 1)


_INS = ['x', 'adj', 'L0_gnn_W', 'L0_gnn_a_l', 'L0_gnn_a_r']
_OUTS = [((8192, 128), 'float32')]


def kernel(**inputs):
    import numpy as _np
    import concourse.bacc as _bacc
    from concourse import mybir as _mybir
    from concourse.bass_utils import run_bass_kernel_spmd as _run

    nc = _bacc.Bacc("TRN2", target_bir_lowering=False, num_devices=1)
    arrays, args = {}, []
    for name in _INS:
        a = _np.ascontiguousarray(inputs[name])
        arrays[f"in_{name}_dram"] = a
        args.append(nc.dram_tensor(f"in_{name}_dram", a.shape, _mybir.dt.from_np(a.dtype), kind="ExternalInput").ap())
    for i, (shape, dtype) in enumerate(_OUTS):
        dt = _mybir.dt.from_np(_np.dtype(dtype))
        args.append(nc.dram_tensor(f"out_{i}_dram", shape, dt, kind="ExternalOutput").ap())
    gat_kernel(nc, *args)
    r = _run(nc, [arrays], core_ids=[0])
    got = tuple(r.results[0][f"out_{i}_dram"] for i in range(len(_OUTS)))
    return got[0]
```

```python
import numpy as np
import concourse.bass as bass
from concourse import mybir
from contextlib import ExitStack


def gat_kernel(nc, x, adj, W, a_l, a_r, out):
    fp32, bf16, fp8, i32 = mybir.dt.float32, mybir.dt.bfloat16, mybir.dt.float8e4, mybir.dt.int32
    ALU, ACT, AX = mybir.AluOpType, mybir.ActivationFunctionType, mybir.AxisListType
    P = 128
    N, D = x.shape
    H, DK = a_l.shape
    SLOPE, EPS = 0.2, 1e-5
    NT = N // P
    J = 4
    CN = J * P
    NCH = N // CN
    PAIRS = 4
    TURNS = NCH // 2
    CP = PAIRS * TURNS
    E = DK + 1
    S3 = 3 * E
    ITEMS = H * J * 2
    PB = 512 // S3
    BANKS = -(-ITEMS // PB)
    DW = D + 2 * H
    BIG = 2.0 ** 100
    ONE8 = 0x38383838
    SHARED = 5216
    VSLOTS = 4

    def on_scalar(k, i):
        return H // 2 + (1 if k == 1 and i == 0 else 0)

    HS = H // 2 + 1

    ctx = ExitStack()
    with ctx:
        def sb(name, shape, dt):
            return ctx.enter_context(nc.sbuf_tensor(name, shape, dt))

        def sem(name):
            return ctx.enter_context(nc.semaphore(name))

        l_dram = nc.dram_tensor("l_scratch", [NCH, H * J, P], fp32, kind="Internal").ap()

        vtab = sb("vtab", [P, NT, 2 * H * S3], bf16)
        abuf = sb("abuf", [P, 2, J, CN], fp32)
        lnext = sb("lnext", [P, H, CN], fp32)
        lrow_s = sb("lrow_s", [P, HS, CN], fp32)
        lrow_v = sb("lrow_v", [P, H - H // 2, CN], fp32)
        MB = H * 2 * CN // 4
        MC = (H - 1) * 2 * CN // 4
        VB = 2 * 2 * H * S3 // 2
        work = sb("work", [P, max(NT * DW, 4 * MB + 2 * MC + 4 * VB)], fp32)
        wh = work[:, 0:NT * DW].rearrange("p (t w) -> p t w", w=DW)
        bmask = work[:, 0:4 * MB].bitcast(fp8).rearrange("p (s h n) -> p s h n", s=4, h=H)
        cmask = work[:, 4 * MB:4 * MB + 2 * MC].bitcast(fp8).rearrange("p (s h n) -> p s h n", s=2, h=H - 1)
        vring = work[:, 4 * MB + 2 * MC:4 * MB + 2 * MC + 4 * VB].bitcast(bf16).rearrange("p (s i e) -> p s i e", s=4, i=2)
        amask = sb("amask", [P, 4, 2 * CN], fp8)
        identf = sb("identf", [P, P], fp32)
        identb = sb("identb", [P, P], bf16)
        w_nat = sb("w_nat", [P, P], fp32)
        w_t = sb("w_t", [P, DW], fp32)
        acol = sb("acol", [P, 2], fp32)
        ablk = sb("ablk", [P, 2 * H], fp32)
        shared = sb("shared", [P, SHARED], fp32)
        used = {"early": 0, "late": 0}

        def carve(when, shape):
            size = int(np.prod(shape))
            at = used[when]
            used[when] += size
            assert used[when] <= SHARED
            names = [f"d{i}" for i in range(len(shape))]
            return shared[:, at:at + size].rearrange(f"p ({' '.join(names)}) -> p {' '.join(names)}",
                                                     **dict(zip(names, shape)))

        def early(*shape):
            return carve("early", shape)

        def late(*shape):
            return carve("late", shape)

        xs = early(2, J, P)
        x_t = early(2, CN)
        used["early"] = (VSLOTS + 2) * 2 * H * 2 * E
        rmax1 = sb("rmax1", [P, H], fp32)
        rmax = sb("rmax", [P, H], fp32)
        rtab = sb("rtab", [P, NT, 2 * H], fp32)
        rring = sb("rring", [P, PAIRS, 2, 2 * H], fp32)
        dr = early(NT, H)
        tl = early(NT, H)
        um = early(2, NT, H)
        lcols = early(NT * H)
        l_t = early(2, P)
        vv = early(NT, H, 2)
        uu = sb("uu", [P, NCH, ITEMS], fp32)
        used["early"] = 0
        vf = early(VSLOTS, 2 * H * 2, E)
        vr = early(2, 2 * H * 2, E)
        acc = late(ITEMS, E)
        dn = sb("dn", [P, ITEMS], fp32)
        den = sb("den", [P, ITEMS // 2], fp32)
        rden = sb("rden", [P, ITEMS // 2], fp32)
        wgt = sb("wgt", [P, ITEMS], fp32)
        pm = late(ITEMS, DK)
        ov = late(J, P)
        mn = late(J, P)
        em = late(J, P)
        zz = late(J, P)
        xr = late(J, P)
        st = sb("st", [P, J, 6], fp32)
        mv = sb("mv", [P, J, 2], fp32)
        epsc = sb("epsc", [P, 2 * J], fp32)
        vrs = sb("vrs", [P, J], fp32)
        yout = late(J, P)

        psum = ctx.enter_context(nc.psum_tensor("psum", [P, BANKS, 512], fp32))
        trp = ctx.enter_context(nc.psum_tensor("trp", [P, 2, CN], bf16))

        consts_zero, consts, w_in, a_in = sem("consts_zero"), sem("consts"), sem("w_in"), sem("a_in")
        w_tr, w_copied, ablk_done, wa_done, wt_done = (sem(s) for s in ("w_tr", "w_copied", "ablk_done", "wa_done", "wt_done"))
        x_in = [sem("x_in0"), sem("x_in1")]
        x_tr, x_copied, wh_done, wh_copied = sem("x_tr"), sem("x_copied"), sem("wh_done"), sem("wh_copied")
        rmax1_done, rmax_done, tab_step, tab_done = sem("rmax1_done"), sem("rmax_done"), sem("tab_step"), sem("tab_done")
        exp_done, l_tr, l_copied, l_stored = sem("exp_done"), sem("l_tr"), sem("l_copied"), sem("l_stored")
        v_prod, v_hi, v_rest, v_mid, v_lo = (sem(s) for s in ("v_prod", "v_hi", "v_rest", "v_mid", "v_lo"))
        a_loaded = [sem("a_loaded0"), sem("a_loaded1")]
        diag_done, tr_done, evac_done = sem("diag_done"), sem("tr_done"), sem("evac_done")
        v_in = [sem(f"v_in{k}") for k in range(PAIRS)]
        r_ready, lrow_act, lrow_dve = sem("r_ready"), sem("lrow_act"), sem("lrow_dve")
        lrow_in, cmp_act, cmp_dve = sem("lrow_in"), sem("cmp_act"), sem("cmp_dve")
        b_ready, c_ready, mm_done, bank_free = sem("b_ready"), sem("c_ready"), sem("mm_done"), sem("bank_free")
        amask_used = sem("amask_used")
        acc_read, dn_step, w_ready = bank_free, sem("dn_step"), sem("w_ready")
        pool_step, mn_ready, em_ready, zz_ready, z_step = (sem(s) for s in ("pool_step", "mn_ready", "em_ready", "zz_ready", "z_step"))
        mv_ready, y_ready, y_stored, xr_in = sem("mv_ready"), sem("y_ready"), sem("y_stored"), sem("xr_in")

        passed = {str(e): sem(f"passed{i}") for i, e in enumerate(
            (nc.sync.engine, nc.tensor.engine, nc.scalar.engine, nc.vector.engine, nc.gpsimd.engine))}
        POOL_STEPS = 5

        block = ctx.enter_context(nc.Block())

        def wait(eng, s, value):
            if not (isinstance(value, int) and value <= 0):
                eng.wait_ge(s, value)

        def repeat(eng, count, body):
            body(0)
            with eng.Fori(1, count) as i:
                body(i)

        def settle(eng):
            eng.sem_inc(passed[str(eng.engine)], 1)

        def group_of(c, t, s):
            return (c + 2 * t + s) & (NCH - 1)

        @block.sync
        def _(sp):
            sp.dma_start(w_nat[:, :], W[:, :]).then_inc(w_in, 16)
            sp.dma_start(acol[:, 0:1], a_l.rearrange("h (k o) -> (h k) o", o=1)).then_inc(a_in, 16)
            sp.dma_start(acol[:, 1:2], a_r.rearrange("h (k o) -> (h k) o", o=1)).then_inc(a_in, 16)

            def x_group(i):
                for s in range(2):
                    g = 2 * i + s
                    wait(sp, x_tr, g - 1)
                    settle(sp)
                    src = x[bass.ds(g * CN, CN), :].rearrange("(j p) d -> p j d", p=P)
                    sp.dma_start(xs[:, s], src).then_inc(x_in[s], 16)

            def a_group(c, t, s):
                q = NCH * c + 2 * t + s
                wait(sp, tr_done, 2 * (q - 1))
                settle(sp)
                col = group_of(c, t, s) * CN
                src = adj[bass.ds(c * CN, CN), bass.ds(col, CN)].rearrange("(j p) m -> p j m", p=P)
                sp.dma_start(abuf[:, s], src).then_inc(a_loaded[s], 16)

            def load_lrow(c):
                src = l_dram[bass.ds(c, 1)].rearrange("o i p -> o (i p)").to_broadcast([P, H * CN])
                sp.dma_start(lnext.rearrange("p h n -> p (h n)"), src).then_inc(lrow_in, 16)

            def loads(c, t):
                for s in range(2):
                    a_group(c, t, s)

            def rest_of_chunk(c, first):
                with sp.Fori(1, 3) as t:
                    loads(c, t)
                sp.wait_ge(lrow_act, c + 1)
                sp.wait_ge(lrow_dve, c + 1)
                settle(sp)
                load_lrow((c + 1) & (NCH - 1))
                wait(sp, zz_ready, c)
                if first:
                    sp.wait_ge(v_lo, NT // 2)
                settle(sp)
                sp.dma_start(xr[:, :], x[bass.ds(c * CN, CN), :].rearrange("(j p) d -> p j d", p=P)).then_inc(xr_in, 16)
                if not first:
                    sp.wait_ge(y_ready, c)
                    settle(sp)
                    store_y(c - 1)
                with sp.Fori(3, TURNS) as t:
                    loads(c, t)

            def store_y(c):
                sp.dma_start(out[bass.ds(c * CN, CN), :].rearrange("(j p) d -> p j d", p=P), yout[:, :]).then_inc(y_stored, 16)

            repeat(sp, NCH // 2, x_group)
            a_group(0, 0, 0)
            a_group(0, 0, 1)
            sp.wait_ge(l_copied, 1)
            sp.dma_start(l_dram.rearrange("(a c) i p -> (c i) a p", a=2), l_t[:, :]).then_inc(l_stored, 16)
            sp.wait_ge(l_stored, 16)
            load_lrow(0)
            rest_of_chunk(0, True)
            with sp.Fori(1, NCH) as c:
                loads(c, 0)
                rest_of_chunk(c, False)
            for s in range(2):
                sp.wait_ge(tr_done, 2 * (NCH * NCH - 1 + s))
                sp.dma_start(abuf[:, s], adj[0:CN, 0:CN].rearrange("(j p) m -> p j m", p=P)).then_inc(a_loaded[s], 16)
            sp.wait_ge(y_ready, NCH)
            store_y(NCH - 1)
            sp.wait_ge(y_stored, 16 * NCH)

        @block.tensor
        def _(pe):
            pe.wait_ge(consts, 2)
            pe.wait_ge(w_in, 16)
            nc.tensor.transpose(psum[:, BANKS - 1, 0:P], w_nat[:, :], identf[:, :]).then_inc(w_tr, 1)
            pe.wait_ge(ablk_done, 1)
            nc.tensor.matmul(psum[:, BANKS - 2, 0:2 * H], w_nat[:, :], ablk[:, :], start=True, stop=True).then_inc(wa_done, 1)
            pe.wait_ge(wt_done, 2)

            def project(i):
                for s in range(2):
                    g = 2 * i + s
                    pe.wait_ge(x_in[s], 16 * (i + 1))
                    wait(pe, x_copied, g - 1)
                    for j in range(J):
                        last = nc.tensor.transpose(psum[:, s, j * P:(j + 1) * P], xs[:, s, j], identf[:, :])
                    last.then_inc(x_tr, 1)
                for s in range(2):
                    g = 2 * i + s
                    pe.wait_ge(x_copied, g + 1)
                    wait(pe, wh_copied, 2 * (g - 1))
                    for j in range(J):
                        last = nc.tensor.matmul(psum[:, 2 + 2 * s + j // 2, (j % 2) * DW:(j % 2 + 1) * DW],
                                                x_t[:, s, j * P:(j + 1) * P], w_t[:, :], start=(j % 2 == 0), stop=True,
                                                skip_group_check=True)
                    last.then_inc(wh_done, 1)

            repeat(pe, NCH // 2, project)
            pe.wait_ge(tab_step, 1)
            for a in range(2):
                last = nc.tensor.transpose(psum[:, BANKS - 1, a * P:(a + 1) * P], lcols[:, a * P:(a + 1) * P], identf[:, :])
            last.then_inc(l_tr, 1)

            def transposes(c, t, k):
                q = 4 * (TURNS * c + t) + k
                kk, tt = k % 4, t + k // 4
                s = kk // 2
                if kk % 2 == 0:
                    pe.wait_ge(a_loaded[s], 16 * (TURNS * c + tt + 1))
                if kk == 0:
                    pe.wait_ge(diag_done, ((TURNS * c + tt) >> 3) + 1)
                wait(pe, evac_done, q)
                for i in range(2):
                    m = (2 * (kk % 2) + i) * P
                    for j in range(J):
                        block_hi = abuf[:, s, j, m:m + P].bitcast(bf16)[:, 1::2]
                        last = nc.tensor.transpose(trp[:, i, j * P:(j + 1) * P], block_hi, identb[:, :])
                last.then_inc(tr_done, 1)

            def products(c, t, k, first_turn):
                q = 4 * (TURNS * c + t) + k
                pe.wait_ge(v_in[k], 16 * (TURNS * c + t + 1))

                def product(mask, i, b, h, j, v):
                    item = (b * H + h) * J + j
                    bank, at = item // PB, item % PB
                    opens = first_turn and k == 0 and i == 0 and at == 0
                    if opens and not isinstance(c, int):
                        pe.wait_ge(bank_free, BANKS * (c - 1) + bank + 1)
                        settle(pe)
                    col = (h * 2 + v) * S3
                    return nc.tensor.matmul(psum[:, bank, at * S3:(at + 1) * S3],
                                            mask[:, i * CN + j * P:i * CN + (j + 1) * P], vring[:, k, i, col:col + S3],
                                            start=opens, stop=True, skip_group_check=True)

                pe.wait_ge(b_ready, q + 1)
                settle(pe)
                for i in range(2):
                    for h in range(H):
                        for j in range(J):
                            product(bmask[:, k, h], i, 0, h, j, 0)
                    for j in range(J):
                        product(bmask[:, k, 0], i, 1, 0, j, 1)
                    for j in range(J):
                        last = product(amask[:, k], i, 1, 0, j, 1)
                last.then_inc(amask_used, 1)
                transposes(c, t, k + 4)
                pe.wait_ge(c_ready, q + 1)
                settle(pe)
                for i in range(2):
                    for h in range(1, H):
                        for j in range(J):
                            last = product(cmask[:, k % 2, h - 1], i, 1, h, j, 1)
                last.then_inc(mm_done, 1)

            def turn(c, t, first_turn):
                for k in range(PAIRS):
                    products(c, t, k, first_turn)

            def chunk(c):
                turn(c, 0, True)
                with pe.Fori(1, TURNS) as t:
                    turn(c, t, False)

            transposes(0, 0, 0)
            transposes(0, 0, 1)
            transposes(0, 0, 2)
            transposes(0, 0, 3)
            pe.wait_ge(v_lo, NT // 2)
            pe.wait_ge(wh_copied, 2 * NCH)
            chunk(0)
            with pe.Fori(1, NCH) as c:
                chunk(c)

        @block.scalar
        def _(act):
            def copy_wh(i):
                for s in range(2):
                    g = 2 * i + s
                    act.wait_ge(wh_done, g + 1)
                    for b in range(2):
                        nc.scalar.copy(wh[:, bass.ds(g * J + 2 * b, 2), :].rearrange("p t w -> p (t w)"),
                                       psum[:, 2 + 2 * s + b, 0:2 * DW]).then_inc(wh_copied, 1)

            repeat(act, NCH // 2, copy_wh)
            act.wait_ge(tab_step, 3)
            for b, scale in enumerate((1.0, SLOPE)):
                nc.scalar.activation(vv[:, :, :, b], dr[:, :, :], ACT.Exp, scale=scale).then_inc(exp_done, 1)
            act.wait_ge(tab_done, 1)
            for b in range(2):
                nc.scalar.activation(uu.rearrange("p c (b h j) -> p c j b h", h=H, b=2)[:, :, :, b],
                                     um[:, b].rearrange("p (c j) h -> p c j h", j=J), ACT.Exp).then_inc(exp_done, 1)

            def split(i):
                def part(s, e, ready, src, done):
                    g = VSLOTS * i + s
                    dst = vtab[:, bass.ds(2 * g, 2), :].rearrange("p t (i e) -> p (t i) e", e=S3)
                    act.wait_ge(ready, g + 1)
                    nc.scalar.copy(dst[:, :, e:e + E], src).then_inc(done, 1)

                for s in range(VSLOTS + 1):
                    if s < VSLOTS:
                        part(s, 0, v_prod, vf[:, s], v_hi)
                    if s >= 1:
                        part(s - 1, E, v_rest, vr[:, (s - 1) % 2], v_mid)

            repeat(act, NT // (2 * VSLOTS), split)

            def evacuate(c, t, k):
                q = 4 * (TURNS * c + t) + k
                act.wait_ge(tr_done, q + 1)
                wait(act, amask_used, q - 3)
                wait(act, c_ready, q - 3)
                settle(act)
                nc.scalar.activation(amask[:, k % 4], trp.rearrange("p i n -> p (i n)"), ACT.Sign,
                                     scale=-1.0, saturate=False).then_inc(evac_done, 1)

            def compare(c, t, k):
                q = 4 * (TURNS * c + t) + k
                t, k = t + k // PAIRS, k % PAIRS
                wait(act, mm_done, q - 3)
                act.wait_ge(r_ready, 2 * (TURNS * c + t) + k // 2 + 1)
                settle(act)
                tile = group_of(c, t, k // 2) * J + 2 * (k % 2)
                act.dma_start(vring[:, k].rearrange("p i e -> p (i e)"),
                              vtab[:, bass.ds(tile, 2)].rearrange("p i e -> p (i e)")).then_inc(v_in[k], 16)
                for i in range(2):
                    for h in range(on_scalar(k, i)):
                        last = nc.scalar.activation(bmask[:, k, h, i * CN:(i + 1) * CN], lrow_s[:, h], ACT.Relu,
                                                    bias=rring[:, k, i, H + h:H + h + 1], scale=BIG, saturate=False)
                last.then_inc(cmp_act, 1)

            def turn(c, t, first=False, last=False):
                for k in range(PAIRS):
                    evacuate(c, t, k + 2)
                    if not (last and k == PAIRS - 1):
                        compare(c, t, k + 1)
                    if first and k == 2 and not isinstance(c, int):
                        elu_exp(c)

            def elu_exp(c):
                act.wait_ge(mn_ready, c)
                nc.scalar.activation(em[:, :], mn[:, :], ACT.Exp).then_inc(em_ready, 1)

            def chunk(c):
                act.wait_ge(lrow_in, 16 * (c + 1))
                wait(act, cmp_act, CP * c)
                nc.scalar.copy(lrow_s[:, :], lnext[:, 0:HS]).then_inc(lrow_act, 1)
                act.wait_ge(lrow_act, c + 1)
                compare(c, 0, 0)
                turn(c, 0, first=True)
                with act.Fori(1, TURNS - 1) as t:
                    turn(c, t)
                turn(c, TURNS - 1, last=True)

            act.wait_ge(tab_done, 2)
            act.wait_ge(v_lo, NT // 2)
            evacuate(0, 0, 0)
            evacuate(0, 0, 1)
            chunk(0)
            with act.Fori(1, NCH) as c:
                chunk(c)
            evacuate(NCH - 1, TURNS - 1, PAIRS + 2)
            elu_exp(NCH)

        @block.vector
        def _(dve):
            dve.wait_ge(consts_zero, 1)
            dve.wait_ge(a_in, 32)
            for h in range(H):
                last = nc.vector.tensor_copy(ablk[h * DK:(h + 1) * DK, h:h + H + 1:H], acol[h * DK:(h + 1) * DK, :])
            last.then_inc(ablk_done, 1)
            dve.wait_ge(w_tr, 1)
            nc.vector.tensor_copy(w_t[:, 0:P], psum[:, BANKS - 1, 0:P]).then_inc(wt_done, 1)
            dve.wait_ge(wa_done, 1)
            nc.vector.tensor_copy(w_t[:, P:DW], psum[:, BANKS - 2, 0:2 * H]).then_inc(wt_done, 1)

            def copy_xt(i):
                for s in range(2):
                    g = 2 * i + s
                    dve.wait_ge(x_tr, g + 1)
                    wait(dve, wh_done, g - 1)
                    nc.vector.tensor_copy(x_t[:, s], psum[:, s, :]).then_inc(x_copied, 1)

            repeat(dve, NCH // 2, copy_xt)
            dve.wait_ge(wh_copied, 2 * NCH)
            l_all, r_all = wh[:, :, D:D + H], wh[:, :, D + H:DW]
            nc.vector.tensor_copy(lcols.rearrange("p (c h j) -> p c h j", h=H, j=J),
                                  l_all.rearrange("p (c j) h -> p c h j", j=J)).then_inc(tab_step, 1)
            nc.vector.tensor_reduce(rmax1[:, :], r_all.rearrange("p t h -> p h t"), AX.X, ALU.max).then_inc(rmax1_done, 1)
            nc.vector.tensor_scalar(rtab[:, :, 0:H], r_all, -1.0, None, ALU.mult).then_inc(tab_step, 1)
            nc.vector.tensor_scalar(rtab[:, :, H:2 * H], r_all, BIG, None, ALU.mult)
            dve.wait_ge(rmax_done, 1)
            r_top = rmax.rearrange("p (o h) -> p o h", o=1).to_broadcast([P, NT, H])
            nc.vector.tensor_tensor(dr[:, :, :], r_all, r_top, ALU.subtract).then_inc(tab_step, 1)
            nc.vector.tensor_tensor(tl[:, :, :], l_all, r_top, ALU.add).then_inc(tab_step, 1)
            dve.wait_ge(tab_step, 4)
            nc.vector.tensor_scalar(um[:, 0], tl[:, :, :], 1.0 - SLOPE, 0.0, ALU.mult, ALU.min)
            nc.vector.tensor_scalar(um[:, 1], tl[:, :, :], SLOPE - 1.0, 0.0, ALU.mult, ALU.min).then_inc(tab_done, 1)
            dve.wait_ge(l_tr, 1)
            nc.vector.tensor_copy(l_t.rearrange("p a n -> p (a n)"), psum[:, BANKS - 1, 0:2 * P]).then_inc(l_copied, 1)

            def split(i):
                for s in range(VSLOTS + 1):
                    if s < VSLOTS:
                        g = VSLOTS * i + s
                        dst = vtab[:, bass.ds(2 * g, 2), :].rearrange("p t (i e) -> p (t i) e", e=S3)
                        dve.wait_ge(v_hi, g + 1)
                        wait(dve, v_lo, g - 1)
                        nc.vector.tensor_tensor(vr[:, s % 2], vf[:, s], dst[:, :, 0:E], ALU.subtract).then_inc(v_rest, 1)
                    if s >= 1:
                        g = VSLOTS * i + s - 1
                        dst = vtab[:, bass.ds(2 * g, 2), :].rearrange("p t (i e) -> p (t i) e", e=S3)
                        dve.wait_ge(v_mid, g + 1)
                        nc.vector.tensor_tensor(dst[:, :, 2 * E:S3], vr[:, (s - 1) % 2], dst[:, :, E:2 * E],
                                                ALU.subtract).then_inc(v_lo, 1)

            repeat(dve, NT // (2 * VSLOTS), split)
            dve.wait_ge(exp_done, 4)
            minus = uu[:, :, ITEMS // 2:ITEMS // 2 + J]
            nc.vector.tensor_scalar(minus, minus, -1.0, None, ALU.mult)
            dve.wait_ge(v_lo, NT // 2)
            nc.vector.memset(epsc[:, 0:J], EPS)
            nc.vector.memset(epsc[:, J:2 * J], -0.5).then_inc(tab_done, 1)

            def words(ap):
                return ap.bitcast(i32)

            def adj_words(k, heads):
                return words(amask[:, k]).rearrange("p (o n) -> p o n", o=1).to_broadcast([P, heads, 2 * CN // 4])

            def compare(c, t, k):
                q = 4 * (TURNS * c + t) + k
                t, k = t + k // PAIRS, k % PAIRS
                wait(dve, mm_done, q - 3)
                dve.wait_ge(r_ready, 2 * (TURNS * c + t) + k // 2 + 1)
                settle(dve)
                for i in range(2):
                    for h in range(on_scalar(k, i), H):
                        last = nc.vector.tensor_scalar(bmask[:, k, h, i * CN:(i + 1) * CN], lrow_v[:, h - H // 2],
                                                       rring[:, k, i, h:h + 1], None, ALU.is_ge, saturate=False)
                last.then_inc(cmp_dve, 1)

            def mask_b(c, t, k):
                q = 4 * (TURNS * c + t) + k
                dve.wait_ge(evac_done, q + 1)
                dve.wait_ge(cmp_act, q + 1)
                dve.wait_ge(cmp_dve, q + 1)
                nc.vector.scalar_tensor_tensor(words(bmask[:, k]), words(bmask[:, k]), ONE8, adj_words(k, H),
                                               ALU.bitwise_and, ALU.bitwise_and).then_inc(b_ready, 1)

            def mask_c(c, t, k):
                q = 4 * (TURNS * c + t) + k
                dve.wait_ge(b_ready, q + 1)
                wait(dve, mm_done, q - 1)
                nc.vector.scalar_tensor_tensor(words(cmask[:, k % 2]), adj_words(k, H - 1), ONE8, words(bmask[:, k, 1:H]),
                                               ALU.bitwise_and, ALU.bitwise_xor).then_inc(c_ready, 1)

            def take_sums(c):
                dve.wait_ge(mm_done, CP * (c + 1))
                if not (isinstance(c, int) and c == 0):
                    dve.wait_ge(pool_step, POOL_STEPS * c)
                for b in range(BANKS):
                    n = min(PB, ITEMS - b * PB)
                    nc.vector.tensor_reduce(acc[:, b * PB:b * PB + n],
                                            psum[:, b, 0:n * S3].rearrange("p (i s e) -> p i e s", s=3, e=E),
                                            AX.X, ALU.add).then_inc(bank_free, 1)
                dve.wait_ge(bank_free, BANKS * (c + 1))
                u_c = uu[:, c] if isinstance(c, int) else uu[:, bass.ds(c, 1)].rearrange("p o i -> p (o i)")
                nc.vector.tensor_tensor(dn[:, :], acc[:, :, DK], u_c, ALU.mult).then_inc(dn_step, 1)
                dve.wait_ge(dn_step, 3 * c + 1)
                nc.vector.tensor_tensor(den[:, :], dn[:, 0:ITEMS // 2], dn[:, ITEMS // 2:ITEMS], ALU.add).then_inc(dn_step, 1)
                dve.wait_ge(dn_step, 3 * c + 2)
                nc.vector.reciprocal(rden[:, :], den[:, :]).then_inc(dn_step, 1)
                dve.wait_ge(dn_step, 3 * c + 3)
                nc.vector.tensor_tensor(wgt.rearrange("p (b i) -> p b i", b=2), u_c.rearrange("p (b i) -> p b i", b=2),
                                        rden.rearrange("p (o i) -> p o i", o=1).to_broadcast([P, 2, ITEMS // 2]),
                                        ALU.mult).then_inc(w_ready, 1)

            def statistics(c):
                dve.wait_ge(em_ready, c + 1)
                dve.wait_ge(zz_ready, c + 1)
                nc.vector.scalar_tensor_tensor(ov[:, :], em[:, :], -1.0, zz[:, :], ALU.add, ALU.add).then_inc(z_step, 1)
                dve.wait_ge(z_step, 2 * c + 1)
                for j in range(J):
                    last = nc.vector.bn_stats(st[:, j], ov[:, j])
                last.then_inc(z_step, 1)
                dve.wait_ge(z_step, 2 * c + 2)
                settle(dve)
                for j in range(J):
                    last = nc.vector.bn_aggr(mv[:, j], st[:, j])
                last.then_inc(mv_ready, 1)

            def turn(c, t, first=False, last=False):
                for k in range(PAIRS):
                    mask_b(c, t, k)
                    if not (last and k == PAIRS - 1):
                        compare(c, t, k + 1)
                    mask_c(c, t, k)
                    if first and not isinstance(c, int):
                        if k == 0:
                            take_sums(c - 1)
                        if k == 3:
                            statistics(c - 1)

            def chunk(c):
                dve.wait_ge(lrow_in, 16 * (c + 1))
                wait(dve, cmp_dve, CP * c)
                nc.vector.tensor_copy(lrow_v[:, :], lnext[:, H // 2:H]).then_inc(lrow_dve, 1)
                dve.wait_ge(lrow_dve, c + 1)
                compare(c, 0, 0)
                turn(c, 0, first=True)
                with dve.Fori(1, TURNS - 1) as t:
                    turn(c, t)
                turn(c, TURNS - 1, last=True)

            chunk(0)
            with dve.Fori(1, NCH) as c:
                chunk(c)
            take_sums(NCH - 1)
            statistics(NCH - 1)

        @block.gpsimd
        def _(pool):
            nc.gpsimd.memset(ablk[:, :], 0.0).then_inc(consts_zero, 1)
            nc.gpsimd.memset(identf[:, :], 0.0).then_inc(consts_zero, 1)
            pool.wait_ge(consts_zero, 2)
            nc.gpsimd.affine_select(out=identf[:, :], in_=identf[:, :], compare_op=ALU.not_equal, fill=1.0, base=0,
                                    pattern=[[-1, P]], channel_multiplier=1).then_inc(consts, 1)
            pool.wait_ge(consts, 1)
            nc.gpsimd.tensor_copy(identb[:, :], identf[:, :]).then_inc(consts, 1)
            pool.wait_ge(rmax1_done, 1)
            nc.gpsimd.partition_all_reduce(rmax[:, :], rmax1[:, :], P, bass.bass_isa.ReduceOp.max).then_inc(rmax_done, 1)

            def product(i):
                for s in range(VSLOTS):
                    g = VSLOTS * i + s
                    wait(pool, v_rest, g - VSLOTS + 1)
                    v4 = vf[:, s].rearrange("p (t h b) e -> p t h b e", t=2, b=2)
                    w3 = wh[:, bass.ds(2 * g, 2), 0:D].rearrange("p t (h d) -> p t h d", h=H)
                    for b in range(2):
                        vb = vv[:, bass.ds(2 * g, 2), :, b]
                        nc.gpsimd.tensor_tensor(v4[:, :, :, b, 0:DK], w3, vb.rearrange("p t (h o) -> p t h o", o=1).to_broadcast([P, 2, H, DK]),
                                                ALU.mult)
                    nc.gpsimd.tensor_copy(vf[:, s, :, DK], vv[:, bass.ds(2 * g, 2)].rearrange("p t h b -> p (t h b)")).then_inc(v_prod, 1)

            pool.wait_ge(exp_done, 2)
            repeat(pool, NT // (2 * VSLOTS), product)

            def add_diagonal(c):
                pool.wait_ge(a_loaded[0], 16 * (TURNS * c + 1))
                row = abuf[:, 0].rearrange("p j n -> p (j n)")
                diag = bass.AP(row.tensor, row.offset, [row.ap[0], [CN + P, J], [1, P]])
                nc.gpsimd.tensor_tensor(diag, diag, identf.rearrange("p (o n) -> p o n", o=1).to_broadcast([P, J, P]),
                                        ALU.add).then_inc(diag_done, 1)

            def scores_of(c, t, groups=(0, 1)):
                for s in groups:
                    free = 4 * (TURNS * c + t) + 2 * s - 2
                    wait(pool, cmp_act, free)
                    wait(pool, cmp_dve, free)
                    settle(pool)
                    nc.gpsimd.tensor_copy(rring[:, 2 * s:2 * s + 2].rearrange("p k i w -> p (k i w)"),
                                          rtab[:, bass.ds(group_of(c, t, s) * J, J)].rearrange("p i w -> p (i w)")).then_inc(r_ready, 1)

            def weigh_sums(c):
                base = POOL_STEPS * c
                pool.wait_ge(w_ready, c + 1)
                nc.gpsimd.tensor_tensor(pm[:, :], acc[:, :, 0:DK],
                                        wgt.rearrange("p (i o) -> p i o", o=1).to_broadcast([P, ITEMS, DK]),
                                        ALU.mult).then_inc(pool_step, 1)
                pool.wait_ge(pool_step, base + 1)
                p2 = pm.rearrange("p (b h j) d -> p b h j d", h=H, b=2)
                nc.gpsimd.tensor_tensor(ov.rearrange("p j (h d) -> p h j d", h=H), p2[:, 0], p2[:, 1],
                                        ALU.add).then_inc(pool_step, 1)
                pool.wait_ge(pool_step, base + 2)
                settle(pool)
                nc.gpsimd.tensor_scalar(mn[:, :], ov[:, :], 0.0, None, ALU.min).then_inc(mn_ready, 1)
                pool.wait_ge(mn_ready, c + 1)
                nc.gpsimd.tensor_tensor(zz[:, :], ov[:, :], mn[:, :], ALU.subtract).then_inc(pool_step, 1)
                pool.wait_ge(pool_step, base + 3)
                pool.wait_ge(xr_in, 16 * (c + 1))
                nc.gpsimd.tensor_tensor(zz[:, :], zz[:, :], xr[:, :], ALU.add).then_inc(zz_ready, 1)

            def normalise(c):
                base = POOL_STEPS * c
                pool.wait_ge(mv_ready, c + 1)
                nc.gpsimd.tensor_tensor(vrs[:, :], mv[:, :, 1], epsc[:, 0:J], ALU.add).then_inc(pool_step, 1)
                pool.wait_ge(pool_step, base + 4)
                nc.gpsimd.tensor_tensor(vrs[:, :], vrs[:, :], epsc[:, J:2 * J], ALU.pow)
                nc.gpsimd.tensor_tensor(pm[:, 0:J * P // DK].rearrange("p (j g) d -> p j (g d)", j=J), ov[:, :],
                                        mv[:, :, 0:1].to_broadcast([P, J, P]), ALU.subtract).then_inc(pool_step, 1)
                pool.wait_ge(pool_step, base + 5)
                if not (isinstance(c, int) and c == 0):
                    pool.wait_ge(y_stored, 16 * c)
                nc.gpsimd.tensor_tensor(yout[:, :], pm[:, 0:J * P // DK].rearrange("p (j g) d -> p j (g d)", j=J),
                                        vrs.rearrange("p (j o) -> p j o", o=1).to_broadcast([P, J, P]),
                                        ALU.mult).then_inc(y_ready, 1)

            pool.wait_ge(tab_done, 1)
            scores_of(0, 0)
            add_diagonal(0)
            with pool.Fori(1, TURNS) as t:
                scores_of(0, t)
            add_diagonal(1)
            with pool.Fori(1, NCH) as c:
                scores_of(c, 0)
                scores_of(c, 1, (0,))
                weigh_sums(c - 1)
                scores_of(c, 1, (1,))
                normalise(c - 1)
                with pool.Fori(2, TURNS) as t:
                    scores_of(c, t)
                add_diagonal(c + 1)
            weigh_sums(NCH - 1)
            normalise(NCH - 1)


_INS = ['x', 'adj', 'L0_gnn_W', 'L0_gnn_a_l', 'L0_gnn_a_r']
_OUTS = [((8192, 128), 'float32')]


def kernel(**inputs):
    import numpy as _np
    import concourse.bacc as _bacc
    from concourse import mybir as _mybir
    from concourse.bass_utils import run_bass_kernel_spmd as _run

    nc = _bacc.Bacc("TRN2", target_bir_lowering=False, num_devices=1)
    arrays, args = {}, []
    for name in _INS:
        a = _np.ascontiguousarray(inputs[name])
        arrays[f"in_{name}_dram"] = a
        args.append(nc.dram_tensor(f"in_{name}_dram", a.shape, _mybir.dt.from_np(a.dtype), kind="ExternalInput").ap())
    for i, (shape, dtype) in enumerate(_OUTS):
        dt = _mybir.dt.from_np(_np.dtype(dtype))
        args.append(nc.dram_tensor(f"out_{i}_dram", shape, dt, kind="ExternalOutput").ap())
    gat_kernel(nc, *args)
    r = _run(nc, [arrays], core_ids=[0])
    got = tuple(r.results[0][f"out_{i}_dram"] for i in range(len(_OUTS)))
    return got[0]
```

```python
import numpy as np
import concourse.bass as bass
from concourse import mybir
from contextlib import ExitStack


def gat_kernel(nc, x, adj, W, a_l, a_r, out):
    fp32, bf16, fp8, i32 = mybir.dt.float32, mybir.dt.bfloat16, mybir.dt.float8e4, mybir.dt.int32
    ALU, ACT, AX = mybir.AluOpType, mybir.ActivationFunctionType, mybir.AxisListType
    P = 128
    N, D = x.shape
    H, DK = a_l.shape
    SLOPE, EPS = 0.2, 1e-5
    NT = N // P
    J = 4
    CN = J * P
    NCH = N // CN
    PAIRS = 4
    TURNS = NCH // 2
    CP = PAIRS * TURNS
    E = DK + 1
    S3 = 3 * E
    ITEMS = H * J * 2
    PB = 512 // S3
    BANKS = -(-ITEMS // PB)
    OPEN_BANKS = -(-(H * J + J) // PB)
    DW = D + 2 * H
    BIG = 2.0 ** 100
    ONE8 = 0x38383838
    SHARED = 5216
    VSLOTS = PAIRS

    def on_scalar(c, t, k, i):
        if is_zero(c) and not is_last(t):
            return H // 2 - (1 if (k, i) in TABLES_FEWER else 0)
        if is_zero(t):
            return H // 2 + (1 if (k, i) in FIRST_EXTRA else 0)
        return H // 2 + (1 if (k, i) in EXTRA else 0)

    def by_sums(c, t, k):
        return 1

    TABLES_FEWER = ((0, 1), (1, 1), (2, 1))
    FIRST_EXTRA = ((0, 0), (1, 0), (2, 0), (3, 0))
    EXTRA = ((1, 0),)

    def is_zero(c):
        return isinstance(c, int) and c == 0

    def is_last(t):
        return isinstance(t, int) and t == TURNS - 1

    ctx = ExitStack()
    with ctx:
        def sb(name, shape, dt):
            return ctx.enter_context(nc.sbuf_tensor(name, shape, dt))

        def sem(name):
            return ctx.enter_context(nc.semaphore(name))

        l_dram = nc.dram_tensor("l_scratch", [NCH, H * J, P], fp32, kind="Internal").ap()

        vtab = sb("vtab", [P, NT, 2 * H * S3], bf16)
        abuf = sb("abuf", [P, 2, J, CN], fp32)
        lrow = sb("lrow", [P, 2, H, CN], fp32)
        MB = H * 2 * CN // 4
        MC = (H - 1) * 2 * CN // 4
        VB = 2 * 2 * H * S3 // 2
        work = sb("work", [P, 4 * MB + 2 * MC + 4 * VB], fp32)
        wh = vtab[:, :, 0:2 * DW].bitcast(fp32)
        bmask = work[:, 0:4 * MB].bitcast(fp8).rearrange("p (s h n) -> p s h n", s=4, h=H)
        cmask = work[:, 4 * MB:4 * MB + 2 * MC].bitcast(fp8).rearrange("p (s h n) -> p s h n", s=2, h=H - 1)
        vring = work[:, 4 * MB + 2 * MC:4 * MB + 2 * MC + 4 * VB].bitcast(bf16).rearrange("p (s i e) -> p s i e", s=4, i=2)
        amask = sb("amask", [P, 4, 2 * CN], fp8)
        identf = sb("identf", [P, P], fp32)
        identb = sb("identb", [P, P], bf16)
        w_nat = sb("w_nat", [P, P], fp32)
        w_t = sb("w_t", [P, DW], fp32)
        acol = sb("acol", [P, 2], fp32)
        ablk = sb("ablk", [P, 2 * H], fp32)
        shared = sb("shared", [P, SHARED], fp32)
        used = {"early": 0, "late": 0}

        def carve(when, shape):
            size = int(np.prod(shape))
            at = used[when]
            used[when] += size
            assert used[when] <= SHARED
            names = [f"d{i}" for i in range(len(shape))]
            return shared[:, at:at + size].rearrange(f"p ({' '.join(names)}) -> p {' '.join(names)}",
                                                     **dict(zip(names, shape)))

        def early(*shape):
            return carve("early", shape)

        def late(*shape):
            return carve("late", shape)

        xs = early(4, J, P)
        x_t = early(2, CN)
        used["early"] = (VSLOTS + 2) * 2 * H * 2 * E
        vv = early(NT, H, 2)
        rmax1 = sb("rmax1", [P, H], fp32)
        rmax = sb("rmax", [P, H], fp32)
        rtab = sb("rtab", [P, NT, 2 * H], fp32)
        rring = sb("rring", [P, PAIRS, 2, 2 * H], fp32)
        dr = early(NT, H)
        tl = early(NT, H)
        um = early(2, NT, H)
        lcols = early(NT * H)
        l_t = early(2, P)
        uu = sb("uu", [P, NCH, ITEMS], fp32)
        used["early"] = 0
        vf = early(VSLOTS, 2 * H * 2, E)
        vr = early(2, 2 * H * 2, E)
        acc = late(ITEMS, E)
        dn = sb("dn", [P, ITEMS], fp32)
        den = sb("den", [P, ITEMS // 2], fp32)
        rden = sb("rden", [P, ITEMS // 2], fp32)
        wgt = sb("wgt", [P, ITEMS], fp32)
        pm = late(ITEMS, DK)
        ov = late(J, P)
        mn = late(J, P)
        em = late(J, P)
        zz = late(J, P)
        assert used["late"] >= (VSLOTS + 2) * 2 * H * 2 * E + NT * H * 2
        xr = late(J, P)
        st = sb("st", [P, J, 6], fp32)
        mv = sb("mv", [P, J, 2], fp32)
        epsc = sb("epsc", [P, 2 * J], fp32)
        vrs = sb("vrs", [P, J], fp32)
        yout = late(J, P)

        psum = ctx.enter_context(nc.psum_tensor("psum", [P, BANKS, 512], fp32))
        trp = ctx.enter_context(nc.psum_tensor("trp", [P, 2, CN], bf16))

        consts_zero, consts, w_in, a_in = sem("consts_zero"), sem("consts"), sem("w_in"), sem("a_in")
        w_tr, w_copied, ablk_done, wa_done, wt_done = (sem(s) for s in ("w_tr", "w_copied", "ablk_done", "wa_done", "wt_done"))
        x_in = [sem(f"x_in{s}") for s in range(4)]
        x_tr, x_copied, wh_done, wh_copied = sem("x_tr"), sem("x_copied"), sem("wh_done"), sem("wh_copied")
        rmax1_done, rmax_done, tab_step, tab_done = sem("rmax1_done"), sem("rmax_done"), sem("tab_step"), sem("tab_done")
        exp_done, l_tr, l_copied, l_stored = sem("exp_done"), sem("l_tr"), sem("l_copied"), sem("l_stored")
        v_prod, v_hi, v_rest, v_mid, v_lo = (sem(s) for s in ("v_prod", "v_hi", "v_rest", "v_mid", "v_lo"))
        a_loaded = [sem("a_loaded0"), sem("a_loaded1")]
        diag_done, tr_done, evac_done = sem("diag_done"), sem("tr_done"), sem("evac_done")
        v_in = [sem(f"v_in{k}") for k in range(PAIRS)]
        r_ready = sem("r_ready")
        lrow_in, cmp_act, cmp_dve = sem("lrow_in"), sem("cmp_act"), sem("cmp_dve")
        b_ready, c_ready, mm_done, bank_free = sem("b_ready"), sem("c_ready"), sem("mm_done"), sem("bank_free")
        amask_used = sem("amask_used")
        acc_read, dn_step, w_ready = bank_free, sem("dn_step"), sem("w_ready")
        pool_step, mn_ready, em_ready, zz_ready, z_step = (sem(s) for s in ("pool_step", "mn_ready", "em_ready", "zz_ready", "z_step"))
        mv_ready, y_ready, y_stored, xr_in = sem("mv_ready"), sem("y_ready"), sem("y_stored"), sem("xr_in")

        passed = {str(e): sem(f"passed{i}") for i, e in enumerate(
            (nc.sync.engine, nc.tensor.engine, nc.scalar.engine, nc.vector.engine, nc.gpsimd.engine))}
        POOL_STEPS = 5

        block = ctx.enter_context(nc.Block())

        def wait(eng, s, value):
            if not (isinstance(value, int) and value <= 0):
                eng.wait_ge(s, value)

        def repeat(eng, count, body):
            body(0)
            with eng.Fori(1, count) as i:
                body(i)

        def settle(eng):
            eng.sem_inc(passed[str(eng.engine)], 1)

        def group_of(c, t, s):
            return (c + 2 * t + s) & (NCH - 1)

        @block.sync
        def _(sp):
            sp.dma_start(w_nat[:, :], W[:, :]).then_inc(w_in, 16)
            sp.dma_start(acol[:, 0:1], a_l.rearrange("h (k o) -> (h k) o", o=1)).then_inc(a_in, 16)
            sp.dma_start(acol[:, 1:2], a_r.rearrange("h (k o) -> (h k) o", o=1)).then_inc(a_in, 16)

            def x_groups(i):
                for s in range(4):
                    g = 4 * i + s
                    wait(sp, x_tr, g - 3)
                    settle(sp)
                    src = x[bass.ds(g * CN, CN), :].rearrange("(j p) d -> p j d", p=P)
                    sp.dma_start(xs[:, s], src).then_inc(x_in[s], 16)

            def a_group(c, t, s):
                q = NCH * c + 2 * t + s
                wait(sp, tr_done, 2 * (q - 1))
                settle(sp)
                col = group_of(c, t, s) * CN
                src = adj[bass.ds(c * CN, CN), bass.ds(col, CN)].rearrange("(j p) m -> p j m", p=P)
                sp.dma_start(abuf[:, s], src).then_inc(a_loaded[s], 16)

            def load_lrow(c):
                src = l_dram[bass.ds(c, 1)].rearrange("o i p -> o (i p)").to_broadcast([P, H * CN])
                dst = lrow[:, bass.ds(c & 1, 1)].rearrange("q o h n -> q (o h n)")
                sp.dma_start(dst, src).then_inc(lrow_in, 16)

            def loads(c, t):
                for s in range(2):
                    a_group(c, t, s)

            def rest_of_chunk(c, first):
                with sp.Fori(1, 3) as t:
                    loads(c, t)
                wait(sp, cmp_act, CP * c)
                wait(sp, cmp_dve, CP * c)
                if not first:
                    settle(sp)
                load_lrow((c + 1) & (NCH - 1))
                wait(sp, zz_ready, c)
                if first:
                    sp.wait_ge(exp_done, 4)
                settle(sp)
                sp.dma_start(xr[:, :], x[bass.ds(c * CN, CN), :].rearrange("(j p) d -> p j d", p=P)).then_inc(xr_in, 16)
                if not first:
                    sp.wait_ge(y_ready, c)
                    settle(sp)
                    store_y(c - 1)
                with sp.Fori(3, TURNS) as t:
                    loads(c, t)

            def store_y(c):
                sp.dma_start(out[bass.ds(c * CN, CN), :].rearrange("(j p) d -> p j d", p=P), yout[:, :]).then_inc(y_stored, 16)

            repeat(sp, NCH // 4, x_groups)
            a_group(0, 0, 0)
            a_group(0, 0, 1)
            sp.wait_ge(l_copied, 1)
            sp.dma_start(l_dram.rearrange("(a c) i p -> (c i) a p", a=2), l_t[:, :]).then_inc(l_stored, 16)
            sp.wait_ge(l_stored, 16)
            load_lrow(0)
            rest_of_chunk(0, True)
            with sp.Fori(1, NCH) as c:
                loads(c, 0)
                rest_of_chunk(c, False)
            for s in range(2):
                sp.wait_ge(tr_done, 2 * (NCH * NCH - 1 + s))
                sp.dma_start(abuf[:, s], adj[0:CN, 0:CN].rearrange("(j p) m -> p j m", p=P)).then_inc(a_loaded[s], 16)
            sp.wait_ge(y_ready, NCH)
            store_y(NCH - 1)
            sp.wait_ge(y_stored, 16 * NCH)

        @block.tensor
        def _(pe):
            pe.wait_ge(consts, 2)
            pe.wait_ge(w_in, 16)
            nc.tensor.transpose(psum[:, BANKS - 1, 0:P], w_nat[:, :], identf[:, :]).then_inc(w_tr, 1)
            pe.wait_ge(ablk_done, 1)
            nc.tensor.matmul(psum[:, BANKS - 2, 0:2 * H], w_nat[:, :], ablk[:, :], start=True, stop=True).then_inc(wa_done, 1)
            pe.wait_ge(wt_done, 2)

            def project(g, s):
                pe.wait_ge(x_copied, g + 1)
                wait(pe, wh_copied, 2 * (g - 1))
                for j in range(J):
                    last = nc.tensor.matmul(psum[:, 2 + 2 * (s % 2) + j // 2, (j % 2) * DW:(j % 2 + 1) * DW],
                                            x_t[:, s % 2, j * P:(j + 1) * P], w_t[:, :], start=(j % 2 == 0), stop=True,
                                            skip_group_check=True)
                last.then_inc(wh_done, 1)

            def project_groups(i):
                for s in range(4):
                    g = 4 * i + s
                    pe.wait_ge(x_in[s], 16 * (i + 1))
                    wait(pe, x_copied, g - 1)
                    for j in range(J):
                        last = nc.tensor.transpose(psum[:, s % 2, j * P:(j + 1) * P], xs[:, s, j], identf[:, :])
                    last.then_inc(x_tr, 1)
                    if not (is_zero(i) and s == 0):
                        project(g - 1, s - 1)

            repeat(pe, NCH // 4, project_groups)
            project(NCH - 1, NCH - 1)
            pe.wait_ge(tab_step, 1)
            for a in range(2):
                last = nc.tensor.transpose(psum[:, BANKS - 1, a * P:(a + 1) * P], lcols[:, a * P:(a + 1) * P], identf[:, :])
            last.then_inc(l_tr, 1)

            def transposes(c, t, k):
                q = 4 * (TURNS * c + t) + k
                kk, tt = k % 4, t + k // 4
                s = kk // 2
                if kk % 2 == 0:
                    pe.wait_ge(a_loaded[s], 16 * (TURNS * c + tt + 1))
                if kk == 0:
                    pe.wait_ge(diag_done, ((TURNS * c + tt) >> 3) + 1)
                wait(pe, evac_done, q)
                for i in range(2):
                    m = (2 * (kk % 2) + i) * P
                    for j in range(J):
                        block_hi = abuf[:, s, j, m:m + P].bitcast(bf16)[:, 1::2]
                        last = nc.tensor.transpose(trp[:, i, j * P:(j + 1) * P], block_hi, identb[:, :])
                last.then_inc(tr_done, 1)

            def products(c, t, k, first_turn):
                q = 4 * (TURNS * c + t) + k
                pe.wait_ge(v_in[k], 16 * (TURNS * c + t + 1))

                heads = by_sums(c, t, k)

                def product(mask, i, b, h, j, v, again=False):
                    item = (b * H + h) * J + j
                    bank, at = item // PB, item % PB
                    opens = first_turn and k == 0 and i == 0 and at == 0 and not again
                    if opens and not isinstance(c, int):
                        pe.wait_ge(bank_free, BANKS * (c - 1) + bank + 1)
                        settle(pe)
                    col = (h * 2 + v) * S3
                    return nc.tensor.matmul(psum[:, bank, at * S3:(at + 1) * S3],
                                            mask[:, i * CN + j * P:i * CN + (j + 1) * P], vring[:, k, i, col:col + S3],
                                            start=opens, stop=True, skip_group_check=True)

                pe.wait_ge(b_ready, q + 1)
                settle(pe)
                for i in range(2):
                    for h in range(H):
                        for j in range(J):
                            product(bmask[:, k, h], i, 0, h, j, 0)
                    for h in range(heads):
                        for j in range(J):
                            product(bmask[:, k, h], i, 1, h, j, 1)
                    for h in range(heads):
                        for j in range(J):
                            last = product(amask[:, k], i, 1, h, j, 1, again=True)
                last.then_inc(amask_used, 1)
                transposes(c, t, k + 4)
                pe.wait_ge(c_ready, q + 1)
                settle(pe)
                for i in range(2):
                    for h in range(heads, H):
                        for j in range(J):
                            last = product(cmask[:, k % 2, h - 1], i, 1, h, j, 1)
                last.then_inc(mm_done, 1)

            def turn(c, t, first_turn):
                for k in range(PAIRS):
                    products(c, t, k, first_turn)

            def chunk(c):
                turn(c, 0, True)
                with pe.Fori(1, TURNS) as t:
                    turn(c, t, False)

            transposes(0, 0, 0)
            transposes(0, 0, 1)
            transposes(0, 0, 2)
            transposes(0, 0, 3)
            pe.wait_ge(wh_copied, 2 * NCH)
            pe.wait_ge(x_copied, NCH)
            pe.wait_ge(l_copied, 1)
            chunk(0)
            with pe.Fori(1, NCH) as c:
                chunk(c)

        @block.scalar
        def _(act):
            def copy_wh(i):
                for s in range(2):
                    g = 2 * i + s
                    act.wait_ge(wh_done, g + 1)
                    for b in range(2):
                        nc.scalar.copy(wh[:, bass.ds(g * J + 2 * b, 2), :],
                                       psum[:, 2 + 2 * s + b, 0:2 * DW].rearrange("p (t w) -> p t w", w=DW)).then_inc(wh_copied, 1)

            repeat(act, NCH // 2, copy_wh)
            act.wait_ge(tab_step, 3)
            for b, scale in enumerate((1.0, SLOPE)):
                nc.scalar.activation(vv[:, :, :, b], dr[:, :, :], ACT.Exp, scale=scale).then_inc(exp_done, 1)
            act.wait_ge(tab_done, 1)
            for b in range(2):
                nc.scalar.activation(uu.rearrange("p c (b h j) -> p c j b h", h=H, b=2)[:, :, :, b],
                                     um[:, b].rearrange("p (c j) h -> p c j h", j=J), ACT.Exp).then_inc(exp_done, 1)

            def part(g, s, e, ready, src, done):
                dst = vtab[:, bass.ds(2 * g, 2), :].rearrange("p t (i e) -> p (t i) e", e=S3)
                act.wait_ge(ready, g + 1)
                nc.scalar.copy(dst[:, :, e:e + E], src).then_inc(done, 1)

            def upper(g, s):
                part(g, s, 0, v_prod, vf[:, s], v_hi)

            def middle(g, s):
                part(g, s, E, v_rest, vr[:, s % 2], v_mid)

            for g in range(VSLOTS):
                upper(g, g)
                if g > 0:
                    middle(g - 1, g - 1)
            middle(VSLOTS - 1, VSLOTS - 1)

            def evacuate(c, t, k):
                q = 4 * (TURNS * c + t) + k
                act.wait_ge(tr_done, q + 1)
                wait(act, amask_used, q - 3)
                wait(act, c_ready, q - 3)
                settle(act)
                nc.scalar.activation(amask[:, k % 4], trp.rearrange("p i n -> p (i n)"), ACT.Sign,
                                     scale=-1.0, saturate=False).then_inc(evac_done, 1)

            def compare(c, parity, t, k):
                q = 4 * (TURNS * c + t) + k
                t, k = t + k // PAIRS, k % PAIRS
                wait(act, mm_done, q - 3)
                act.wait_ge(r_ready, 2 * (TURNS * c + t) + k // 2 + 1)
                settle(act)
                if is_zero(c):
                    act.wait_ge(v_lo, q + 1)
                    settle(act)
                tile = group_of(c, t, k // 2) * J + 2 * (k % 2)
                act.dma_start(vring[:, k].rearrange("p i e -> p (i e)"),
                              vtab[:, bass.ds(tile, 2)].rearrange("p i e -> p (i e)")).then_inc(v_in[k], 16)
                for i in range(2):
                    for h in range(on_scalar(c, t, k, i)):
                        last = nc.scalar.activation(bmask[:, k, h, i * CN:(i + 1) * CN], lrow[:, parity, h], ACT.Relu,
                                                    bias=rring[:, k, i, H + h:H + h + 1], scale=BIG, saturate=False)
                last.then_inc(cmp_act, 1)

            def turn(c, parity, t, first=False, second=False, last=False):
                for k in range(PAIRS):
                    q = PAIRS * t + k
                    if is_zero(c) and not (isinstance(q, int) and (q == 0 or q + 3 >= CP)):
                        middle(q + 3, (k + 3) % PAIRS)
                    if is_zero(c) and not last:
                        for s in ((0, 1), (2,), (3,), ())[k]:
                            upper(PAIRS * (t + 1) + s, s)
                    evacuate(c, t, k + 2)
                    if not (last and k == PAIRS - 1):
                        compare(c, parity, t, k + 1)
                    if second and k == 0 and not is_zero(c):
                        elu_exp(c)

            def elu_exp(c):
                act.wait_ge(mn_ready, c)
                nc.scalar.activation(em[:, :], mn[:, :], ACT.Exp).then_inc(em_ready, 1)

            def chunk(c, parity):
                act.wait_ge(lrow_in, 16 * (c + 1))
                compare(c, parity, 0, 0)
                turn(c, parity, 0, first=True)
                turn(c, parity, 1, second=True)
                with act.Fori(2, TURNS - 1) as t:
                    turn(c, parity, t)
                turn(c, parity, TURNS - 1, last=True)

            act.wait_ge(tab_done, 2)
            evacuate(0, 0, 0)
            evacuate(0, 0, 1)
            chunk(0, 0)
            with act.Fori(1, NCH - 1, 2) as c:
                chunk(c, 1)
                chunk(c + 1, 0)
            chunk(NCH - 1, 1)
            evacuate(NCH - 1, TURNS - 1, PAIRS + 2)
            elu_exp(NCH)

        @block.vector
        def _(dve):
            dve.wait_ge(consts_zero, 1)
            dve.wait_ge(a_in, 32)
            for h in range(H):
                last = nc.vector.tensor_copy(ablk[h * DK:(h + 1) * DK, h:h + H + 1:H], acol[h * DK:(h + 1) * DK, :])
            last.then_inc(ablk_done, 1)
            dve.wait_ge(w_tr, 1)
            nc.vector.tensor_copy(w_t[:, 0:P], psum[:, BANKS - 1, 0:P]).then_inc(wt_done, 1)
            dve.wait_ge(wa_done, 1)
            nc.vector.tensor_copy(w_t[:, P:DW], psum[:, BANKS - 2, 0:2 * H]).then_inc(wt_done, 1)

            def copy_xt(i):
                for s in range(2):
                    g = 2 * i + s
                    dve.wait_ge(x_tr, g + 1)
                    wait(dve, wh_done, g - 1)
                    nc.vector.tensor_copy(x_t[:, s], psum[:, s, :]).then_inc(x_copied, 1)

            repeat(dve, NCH // 2, copy_xt)
            dve.wait_ge(wh_copied, 2 * NCH)
            l_all, r_all = wh[:, :, D:D + H], wh[:, :, D + H:DW]
            nc.vector.tensor_copy(lcols.rearrange("p (c h j) -> p c h j", h=H, j=J),
                                  l_all.rearrange("p (c j) h -> p c h j", j=J)).then_inc(tab_step, 1)
            nc.vector.tensor_reduce(rmax1[:, :], r_all.rearrange("p t h -> p h t"), AX.X, ALU.max).then_inc(rmax1_done, 1)
            nc.vector.tensor_scalar(rtab[:, :, 0:H], r_all, -1.0, None, ALU.mult).then_inc(tab_step, 1)
            nc.vector.tensor_scalar(rtab[:, :, H:2 * H], r_all, BIG, None, ALU.mult)
            dve.wait_ge(rmax_done, 1)
            r_top = rmax.rearrange("p (o h) -> p o h", o=1).to_broadcast([P, NT, H])
            nc.vector.tensor_tensor(dr[:, :, :], r_all, r_top, ALU.subtract).then_inc(tab_step, 1)
            nc.vector.tensor_tensor(tl[:, :, :], l_all, r_top, ALU.add).then_inc(tab_step, 1)
            dve.wait_ge(tab_step, 4)
            nc.vector.tensor_scalar(um[:, 0], tl[:, :, :], 1.0 - SLOPE, 0.0, ALU.mult, ALU.min)
            nc.vector.tensor_scalar(um[:, 1], tl[:, :, :], SLOPE - 1.0, 0.0, ALU.mult, ALU.min).then_inc(tab_done, 1)
            dve.wait_ge(l_tr, 1)
            nc.vector.tensor_copy(l_t.rearrange("p a n -> p (a n)"), psum[:, BANKS - 1, 0:2 * P]).then_inc(l_copied, 1)

            def lowest(g):
                dst = vtab[:, 2 * g:2 * g + 2, :].rearrange("p t (i e) -> p (t i) e", e=S3)
                dve.wait_ge(v_mid, g + 1)
                nc.vector.tensor_tensor(dst[:, :, 2 * E:S3], vr[:, g % 2], dst[:, :, E:2 * E], ALU.subtract).then_inc(v_lo, 1)

            for g in range(VSLOTS):
                dst = vtab[:, 2 * g:2 * g + 2, :].rearrange("p t (i e) -> p (t i) e", e=S3)
                dve.wait_ge(v_hi, g + 1)
                wait(dve, v_lo, g - 1)
                nc.vector.tensor_tensor(vr[:, g % 2], vf[:, g], dst[:, :, 0:E], ALU.subtract).then_inc(v_rest, 1)
                if g > 0:
                    lowest(g - 1)
            lowest(VSLOTS - 1)
            dve.wait_ge(exp_done, 4)
            minus = uu[:, :, ITEMS // 2:ITEMS]
            nc.vector.tensor_scalar(minus, minus, -1.0, None, ALU.mult)
            nc.vector.memset(epsc[:, 0:J], EPS)
            nc.vector.memset(epsc[:, J:2 * J], -0.5).then_inc(tab_done, 1)

            def words(ap):
                return ap.bitcast(i32)

            def adj_words(k, heads):
                return words(amask[:, k]).rearrange("p (o n) -> p o n", o=1).to_broadcast([P, heads, 2 * CN // 4])

            def compare(c, parity, t, k):
                q = 4 * (TURNS * c + t) + k
                t, k = t + k // PAIRS, k % PAIRS
                wait(dve, mm_done, q - 3)
                dve.wait_ge(r_ready, 2 * (TURNS * c + t) + k // 2 + 1)
                settle(dve)
                for i in range(2):
                    for h in range(on_scalar(c, t, k, i), H):
                        last = nc.vector.tensor_scalar(bmask[:, k, h, i * CN:(i + 1) * CN], lrow[:, parity, h],
                                                       rring[:, k, i, h:h + 1], None, ALU.is_ge, saturate=False)
                last.then_inc(cmp_dve, 1)

            def mask_b(c, t, k):
                q = 4 * (TURNS * c + t) + k
                dve.wait_ge(evac_done, q + 1)
                dve.wait_ge(cmp_act, q + 1)
                dve.wait_ge(cmp_dve, q + 1)
                nc.vector.scalar_tensor_tensor(words(bmask[:, k]), words(bmask[:, k]), ONE8, adj_words(k, H),
                                               ALU.bitwise_and, ALU.bitwise_and).then_inc(b_ready, 1)

            def mask_c(c, t, k):
                heads = by_sums(c, t, k)
                q = 4 * (TURNS * c + t) + k
                dve.wait_ge(b_ready, q + 1)
                wait(dve, mm_done, q - 1)
                nc.vector.tensor_tensor(words(cmask[:, k % 2, heads - 1:H - 1]), adj_words(k, H - heads),
                                        words(bmask[:, k, heads:H]), ALU.bitwise_xor).then_inc(c_ready, 1)

            def take_first_sums(c):
                dve.wait_ge(amask_used, CP * (c + 1))
                if not is_zero(c):
                    dve.wait_ge(pool_step, POOL_STEPS * c)
                add_parts(range(OPEN_BANKS))

            def take_last_sums(c):
                dve.wait_ge(mm_done, CP * (c + 1))
                add_parts(range(OPEN_BANKS, BANKS))

            def add_parts(banks):
                for b in banks:
                    n = min(PB, ITEMS - b * PB)
                    nc.vector.tensor_reduce(acc[:, b * PB:b * PB + n],
                                            psum[:, b, 0:n * S3].rearrange("p (i s e) -> p i e s", s=3, e=E),
                                            AX.X, ALU.add).then_inc(bank_free, 1)

            def weights(c):
                dve.wait_ge(bank_free, BANKS * (c + 1))
                u_c = uu[:, c] if isinstance(c, int) else uu[:, bass.ds(c, 1)].rearrange("p o i -> p (o i)")
                nc.vector.tensor_tensor(dn[:, :], acc[:, :, DK], u_c, ALU.mult).then_inc(dn_step, 1)
                dve.wait_ge(dn_step, 3 * c + 1)
                nc.vector.tensor_tensor(den[:, :], dn[:, 0:ITEMS // 2], dn[:, ITEMS // 2:ITEMS], ALU.add).then_inc(dn_step, 1)
                dve.wait_ge(dn_step, 3 * c + 2)
                nc.vector.reciprocal(rden[:, :], den[:, :]).then_inc(dn_step, 1)
                dve.wait_ge(dn_step, 3 * c + 3)
                nc.vector.tensor_tensor(wgt.rearrange("p (b i) -> p b i", b=2), u_c.rearrange("p (b i) -> p b i", b=2),
                                        rden.rearrange("p (o i) -> p o i", o=1).to_broadcast([P, 2, ITEMS // 2]),
                                        ALU.mult).then_inc(w_ready, 1)

            def statistics(c):
                dve.wait_ge(em_ready, c + 1)
                dve.wait_ge(zz_ready, c + 1)
                nc.vector.scalar_tensor_tensor(ov[:, :], em[:, :], -1.0, zz[:, :], ALU.add, ALU.add).then_inc(z_step, 1)
                dve.wait_ge(z_step, 2 * c + 1)
                for j in range(J):
                    last = nc.vector.bn_stats(st[:, j], ov[:, j])
                last.then_inc(z_step, 1)
                dve.wait_ge(z_step, 2 * c + 2)
                settle(dve)
                for j in range(J):
                    last = nc.vector.bn_aggr(mv[:, j], st[:, j])
                last.then_inc(mv_ready, 1)

            def turn(c, parity, t, first=False, second=False, last=False):
                after = first and not is_zero(c)
                for k in range(PAIRS):
                    mask_b(c, t, k)
                    if after and k == 2:
                        weights(c - 1)
                    if not (last and k == PAIRS - 1):
                        compare(c, parity, t, k + 1)
                    elif not (isinstance(c, int) and c == NCH - 1):
                        first_compare(c + 1, 1 - parity)
                    if after and k == 0:
                        take_first_sums(c - 1)
                    mask_c(c, t, k)
                    if after and k == 0:
                        take_last_sums(c - 1)
                    if second and k == 1 and not is_zero(c):
                        statistics(c - 1)

            def first_compare(c, parity):
                dve.wait_ge(lrow_in, 16 * (c + 1))
                compare(c, parity, 0, 0)

            def chunk(c, parity):
                turn(c, parity, 0, first=True)
                turn(c, parity, 1, second=True)
                with dve.Fori(2, TURNS - 1) as t:
                    turn(c, parity, t)
                turn(c, parity, TURNS - 1, last=True)

            first_compare(0, 0)
            chunk(0, 0)
            with dve.Fori(1, NCH - 1, 2) as c:
                chunk(c, 1)
                chunk(c + 1, 0)
            chunk(NCH - 1, 1)
            take_first_sums(NCH - 1)
            take_last_sums(NCH - 1)
            weights(NCH - 1)
            statistics(NCH - 1)

        @block.gpsimd
        def _(pool):
            nc.gpsimd.memset(ablk[:, :], 0.0).then_inc(consts_zero, 1)
            nc.gpsimd.memset(identf[:, :], 0.0).then_inc(consts_zero, 1)
            pool.wait_ge(consts_zero, 2)
            nc.gpsimd.affine_select(out=identf[:, :], in_=identf[:, :], compare_op=ALU.not_equal, fill=1.0, base=0,
                                    pattern=[[-1, P]], channel_multiplier=1).then_inc(consts, 1)
            pool.wait_ge(consts, 1)
            nc.gpsimd.tensor_copy(identb[:, :], identf[:, :]).then_inc(consts, 1)
            pool.wait_ge(rmax1_done, 1)
            nc.gpsimd.partition_all_reduce(rmax[:, :], rmax1[:, :], P, bass.bass_isa.ReduceOp.max).then_inc(rmax_done, 1)

            def weigh_wh(g, s, b):
                v4 = vf[:, s].rearrange("p (t h b) e -> p t h b e", t=2, b=2)
                w3 = wh[:, bass.ds(2 * g, 2), 0:D].rearrange("p t (h d) -> p t h d", h=H)
                vb = vv[:, bass.ds(2 * g, 2), :, b].rearrange("p t (h o) -> p t h o", o=1).to_broadcast([P, 2, H, DK])
                nc.gpsimd.tensor_tensor(v4[:, :, :, b, 0:DK], w3, vb, ALU.mult)

            def weigh_one(g, s):
                nc.gpsimd.tensor_copy(vf[:, s, :, DK],
                                      vv[:, bass.ds(2 * g, 2)].rearrange("p t h b -> p (t h b)")).then_inc(v_prod, 1)

            def product(g, s):
                weigh_wh(g, s, 0)
                weigh_wh(g, s, 1)
                weigh_one(g, s)

            def add_diagonal(c):
                pool.wait_ge(a_loaded[0], 16 * (TURNS * c + 1))
                row = abuf[:, 0].rearrange("p j n -> p (j n)")
                diag = bass.AP(row.tensor, row.offset, [row.ap[0], [CN + P, J], [1, P]])
                nc.gpsimd.tensor_tensor(diag, diag, identf.rearrange("p (o n) -> p o n", o=1).to_broadcast([P, J, P]),
                                        ALU.add).then_inc(diag_done, 1)

            def scores_of(c, t, groups=(0, 1)):
                for s in groups:
                    free = 4 * (TURNS * c + t) + 2 * s - 2
                    wait(pool, cmp_act, free)
                    wait(pool, cmp_dve, free)
                    settle(pool)
                    nc.gpsimd.tensor_copy(rring[:, 2 * s:2 * s + 2].rearrange("p k i w -> p (k i w)"),
                                          rtab[:, bass.ds(group_of(c, t, s) * J, J)].rearrange("p i w -> p (i w)")).then_inc(r_ready, 1)

            def make_tables(t, first=False, last=False):
                for k in range(PAIRS):
                    g = PAIRS * t + k
                    dst = vtab[:, bass.ds(2 * g, 2), :].rearrange("p t (i e) -> p (t i) e", e=S3)
                    pool.wait_ge(v_hi, g + 1)
                    pool.wait_ge(v_lo, g - 1)
                    settle(pool)
                    nc.gpsimd.tensor_tensor(vr[:, k % 2], vf[:, k], dst[:, :, 0:E], ALU.subtract).then_inc(v_rest, 1)
                    if not (first and k == 0):
                        lowest(g - 1, (k - 1) % PAIRS)
                    if k % 2 == 1:
                        scores_of(0, t, (k // 2,))
                    if not (last and k >= PAIRS - 2):
                        pool.wait_ge(v_rest, g - 1)
                        product(g + 2, (k + 2) % PAIRS)

            def lowest(g, s):
                dst = vtab[:, bass.ds(2 * g, 2), :].rearrange("p t (i e) -> p (t i) e", e=S3)
                pool.wait_ge(v_mid, g + 1)
                settle(pool)
                nc.gpsimd.tensor_tensor(dst[:, :, 2 * E:S3], vr[:, s % 2], dst[:, :, E:2 * E], ALU.subtract).then_inc(v_lo, 1)

            def weigh_sums(c):
                base = POOL_STEPS * c
                pool.wait_ge(w_ready, c + 1)
                nc.gpsimd.tensor_tensor(pm[:, :], acc[:, :, 0:DK],
                                        wgt.rearrange("p (i o) -> p i o", o=1).to_broadcast([P, ITEMS, DK]),
                                        ALU.mult).then_inc(pool_step, 1)
                pool.wait_ge(pool_step, base + 1)
                p2 = pm.rearrange("p (b h j) d -> p b h j d", h=H, b=2)
                nc.gpsimd.tensor_tensor(ov.rearrange("p j (h d) -> p h j d", h=H), p2[:, 0], p2[:, 1],
                                        ALU.add).then_inc(pool_step, 1)
                pool.wait_ge(pool_step, base + 2)
                settle(pool)
                nc.gpsimd.tensor_scalar(mn[:, :], ov[:, :], 0.0, None, ALU.min).then_inc(mn_ready, 1)
                pool.wait_ge(mn_ready, c + 1)
                nc.gpsimd.tensor_tensor(zz[:, :], ov[:, :], mn[:, :], ALU.subtract).then_inc(pool_step, 1)
                pool.wait_ge(pool_step, base + 3)
                pool.wait_ge(xr_in, 16 * (c + 1))
                nc.gpsimd.tensor_tensor(zz[:, :], zz[:, :], xr[:, :], ALU.add).then_inc(zz_ready, 1)

            def normalise(c):
                base = POOL_STEPS * c
                pool.wait_ge(mv_ready, c + 1)
                nc.gpsimd.tensor_tensor(vrs[:, :], mv[:, :, 1], epsc[:, 0:J], ALU.add).then_inc(pool_step, 1)
                pool.wait_ge(pool_step, base + 4)
                nc.gpsimd.tensor_tensor(vrs[:, :], vrs[:, :], epsc[:, J:2 * J], ALU.pow)
                nc.gpsimd.tensor_tensor(pm[:, 0:J * P // DK].rearrange("p (j g) d -> p j (g d)", j=J), ov[:, :],
                                        mv[:, :, 0:1].to_broadcast([P, J, P]), ALU.subtract).then_inc(pool_step, 1)
                pool.wait_ge(pool_step, base + 5)
                if not (isinstance(c, int) and c == 0):
                    pool.wait_ge(y_stored, 16 * c)
                nc.gpsimd.tensor_tensor(yout[:, :], pm[:, 0:J * P // DK].rearrange("p (j g) d -> p j (g d)", j=J),
                                        vrs.rearrange("p (j o) -> p j o", o=1).to_broadcast([P, J, P]),
                                        ALU.mult).then_inc(y_ready, 1)

            add_diagonal(0)
            pool.wait_ge(exp_done, 2)
            for g in range(VSLOTS):
                product(g, g)
            pool.wait_ge(tab_done, 1)
            scores_of(0, 0)
            for s in range(2):
                pool.wait_ge(v_rest, s + 1)
                product(VSLOTS + s, s)
            pool.wait_ge(v_lo, VSLOTS)
            make_tables(1, first=True)
            with pool.Fori(2, TURNS - 1) as t:
                make_tables(t)
            make_tables(TURNS - 1, last=True)
            lowest(NT // 2 - 1, PAIRS - 1)
            add_diagonal(1)
            with pool.Fori(1, NCH) as c:
                scores_of(c, 0)
                scores_of(c, 1, (0,))
                weigh_sums(c - 1)
                scores_of(c, 1, (1,))
                scores_of(c, 2, (0,))
                normalise(c - 1)
                scores_of(c, 2, (1,))
                with pool.Fori(3, TURNS) as t:
                    scores_of(c, t)
                add_diagonal(c + 1)
            weigh_sums(NCH - 1)
            normalise(NCH - 1)


_INS = ['x', 'adj', 'L0_gnn_W', 'L0_gnn_a_l', 'L0_gnn_a_r']
_OUTS = [((8192, 128), 'float32')]


def kernel(**inputs):
    import numpy as _np
    import concourse.bacc as _bacc
    from concourse import mybir as _mybir
    from concourse.bass_utils import run_bass_kernel_spmd as _run

    nc = _bacc.Bacc("TRN2", target_bir_lowering=False, num_devices=1)
    arrays, args = {}, []
    for name in _INS:
        a = _np.ascontiguousarray(inputs[name])
        arrays[f"in_{name}_dram"] = a
        args.append(nc.dram_tensor(f"in_{name}_dram", a.shape, _mybir.dt.from_np(a.dtype), kind="ExternalInput").ap())
    for i, (shape, dtype) in enumerate(_OUTS):
        dt = _mybir.dt.from_np(_np.dtype(dtype))
        args.append(nc.dram_tensor(f"out_{i}_dram", shape, dt, kind="ExternalOutput").ap())
    gat_kernel(nc, *args)
    r = _run(nc, [arrays], core_ids=[0])
    got = tuple(r.results[0][f"out_{i}_dram"] for i in range(len(_OUTS)))
    return got[0]
```
